# Optimizing a Trainium2 kernel written in Bass

```python
import numpy as np
import jax
import jax.numpy as jnp

def _softmax(x, axis=-1):
    return jax.nn.softmax(x, axis=axis)

def _gelu(x):
    return jax.nn.gelu(x, approximate=True)

def _silu(x):
    return jax.nn.silu(x)

def _sigmoid(x):
    return jax.nn.sigmoid(x)

def _layernorm(x, axis=-1, eps=1e-05):
    m = jnp.mean(x, axis=axis, keepdims=True)
    v = jnp.var(x, axis=axis, keepdims=True)
    return (x - m) / jnp.sqrt(v + eps)

def _scatter_add(tgt, idx, src, axis=0):
    return tgt.at[idx].add(src)

def _segment_sum(src, seg, n):
    return jax.ops.segment_sum(src, seg, n)
kernel_name = 'mk_prb_d1_jaxref_r4_20470c'

def setup_inputs(seed: int=0):
    np.random.seed(seed)
    _w = jnp.asarray

    def _L0_attn_setup():
        import math
        import jax, jax.numpy as jnp
        import numpy as np
        N_HEADS = 16
        NUM_BUCKETS = 32
        MAX_DISTANCE = 128
        ROTARY_BASE = 10000.0

        def rotate_half(x):
            x1, x2 = jnp.split(x, 2, axis=-1)
            return jnp.concatenate((-x2, x1), axis=-1)

        def rotary_freqs(T, dim):
            inv_freq = 1.0 / ROTARY_BASE ** (jnp.arange(0, dim, 2, dtype=jnp.float32) / dim)
            t = jnp.arange(T, dtype=jnp.float32)
            freqs = jnp.einsum('i,j->ij', t, inv_freq)
            return jnp.concatenate((freqs, freqs), axis=-1)

        def rel_pos_bucket_causal(rel_pos, num_buckets=NUM_BUCKETS, max_distance=MAX_DISTANCE):
            n = jnp.maximum(-rel_pos, 0)
            max_exact = num_buckets // 2
            is_small = n < max_exact
            n_safe = jnp.maximum(n, 1).astype(jnp.float32)
            val_if_large = max_exact + (jnp.log(n_safe / max_exact) / math.log(max_distance / max_exact) * (num_buckets - max_exact)).astype(jnp.int32)
            val_if_large = jnp.minimum(val_if_large, num_buckets - 1)
            return jnp.where(is_small, n, val_if_large)
        key = jax.random.key(seed)
        ks = jax.random.split(key, 10)
        B, T, C = (2, 512, 256)
        s = 0.02
        return {'x': jax.random.normal(ks[0], (B, T, C), dtype=jnp.float32), 'Wq': jax.random.normal(ks[1], (C, C), dtype=jnp.float32) * s, 'bq': jnp.zeros((C,), dtype=jnp.float32), 'Wk': jax.random.normal(ks[2], (C, C), dtype=jnp.float32) * s, 'bk': jnp.zeros((C,), dtype=jnp.float32), 'Wv': jax.random.normal(ks[3], (C, C), dtype=jnp.float32) * s, 'bv': jnp.zeros((C,), dtype=jnp.float32), 'Wp': jax.random.normal(ks[4], (C, C), dtype=jnp.float32) * s, 'bp': jnp.zeros((C,), dtype=jnp.float32), 'rel_bias_table': jax.random.normal(ks[5], (NUM_BUCKETS, N_HEADS), dtype=jnp.float32) * s}
    _L0_attn_in = _L0_attn_setup()

    def _L0_ffn_setup():
        import jax, jax.numpy as jnp
        import numpy as np
        NUM_COLUMNS = 16
        INPUT_DIM = 256
        NUM_NEURONS = 64
        SPARSITY = 0.05
        B, S = (4, 512)

        def _l2norm(v, axis=-1, eps=1e-12):
            n = jnp.sqrt(jnp.sum(v * v, axis=axis, keepdims=True))
            return v / jnp.maximum(n, eps)
        key = jax.random.key(seed)
        ks = jax.random.split(key, 12)
        D, C, N = (INPUT_DIM, NUM_COLUMNS, NUM_NEURONS)
        inp = {'x': jax.random.normal(ks[0], (B, S, D), dtype=jnp.float32), 'col_emb': jax.random.normal(ks[1], (C, D), dtype=jnp.float32) * 0.02, 'gate_w1': jax.random.normal(ks[2], (D, D // 2), dtype=jnp.float32) / np.sqrt(D), 'gate_b1': jnp.zeros((D // 2,), dtype=jnp.float32), 'gate_w2': jax.random.normal(ks[3], (D // 2, C), dtype=jnp.float32) / np.sqrt(D // 2), 'gate_b2': jnp.zeros((C,), dtype=jnp.float32), 'W_cols': jax.random.normal(ks[4], (C, D, N), dtype=jnp.float32) / np.sqrt(D), 'b_cols': jnp.zeros((C, N), dtype=jnp.float32), 'proj_w': jax.random.normal(ks[5], (C * N, D), dtype=jnp.float32) / np.sqrt(C * N), 'proj_b': jnp.zeros((D,), dtype=jnp.float32), 'ln_g': jnp.ones((D,), dtype=jnp.float32), 'ln_b': jnp.zeros((D,), dtype=jnp.float32)}
        return inp
    _L0_ffn_in = _L0_ffn_setup()
    _d = {'L0_attn_x': _L0_attn_in['x'], 'L0_attn_Wq': _L0_attn_in['Wq'], 'L0_attn_bq': _L0_attn_in['bq'], 'L0_attn_Wk': _L0_attn_in['Wk'], 'L0_attn_bk': _L0_attn_in['bk'], 'L0_attn_Wv': _L0_attn_in['Wv'], 'L0_attn_bv': _L0_attn_in['bv'], 'L0_attn_Wp': _L0_attn_in['Wp'], 'L0_attn_bp': _L0_attn_in['bp'], 'L0_attn_rel_bias_table': _L0_attn_in['rel_bias_table'], 'L0_ffn_col_emb': _L0_ffn_in['col_emb'], 'L0_ffn_gate_w1': _L0_ffn_in['gate_w1'], 'L0_ffn_gate_b1': _L0_ffn_in['gate_b1'], 'L0_ffn_gate_w2': _L0_ffn_in['gate_w2'], 'L0_ffn_gate_b2': _L0_ffn_in['gate_b2'], 'L0_ffn_W_cols': _L0_ffn_in['W_cols'], 'L0_ffn_b_cols': _L0_ffn_in['b_cols'], 'L0_ffn_proj_w': _L0_ffn_in['proj_w'], 'L0_ffn_proj_b': _L0_ffn_in['proj_b'], 'L0_ffn_ln_g': _L0_ffn_in['ln_g'], 'L0_ffn_ln_b': _L0_ffn_in['ln_b']}
    _x0 = _d['L0_attn_x']
    _d['L0_attn_x'] = jax.random.normal(jax.random.fold_in(jax.random.key(seed), 1), (8, 1024, 256), dtype=_x0.dtype)
    del _x0
    return _d

def reference(L0_attn_x, L0_attn_Wq, L0_attn_bq, L0_attn_Wk, L0_attn_bk, L0_attn_Wv, L0_attn_bv, L0_attn_Wp, L0_attn_bp, L0_attn_rel_bias_table, L0_ffn_col_emb, L0_ffn_gate_w1, L0_ffn_gate_b1, L0_ffn_gate_w2, L0_ffn_gate_b2, L0_ffn_W_cols, L0_ffn_b_cols, L0_ffn_proj_w, L0_ffn_proj_b, L0_ffn_ln_g, L0_ffn_ln_b):

    def _L0_attn_ref(x, Wq, bq, Wk, bk, Wv, bv, Wp, bp, rel_bias_table):
        import math
        import jax, jax.numpy as jnp
        import numpy as np
        N_HEADS = 16
        NUM_BUCKETS = 32
        MAX_DISTANCE = 128
        ROTARY_BASE = 10000.0

        def rotate_half(x):
            x1, x2 = jnp.split(x, 2, axis=-1)
            return jnp.concatenate((-x2, x1), axis=-1)

        def rotary_freqs(T, dim):
            inv_freq = 1.0 / ROTARY_BASE ** (jnp.arange(0, dim, 2, dtype=jnp.float32) / dim)
            t = jnp.arange(T, dtype=jnp.float32)
            freqs = jnp.einsum('i,j->ij', t, inv_freq)
            return jnp.concatenate((freqs, freqs), axis=-1)

        def rel_pos_bucket_causal(rel_pos, num_buckets=NUM_BUCKETS, max_distance=MAX_DISTANCE):
            n = jnp.maximum(-rel_pos, 0)
            max_exact = num_buckets // 2
            is_small = n < max_exact
            n_safe = jnp.maximum(n, 1).astype(jnp.float32)
            val_if_large = max_exact + (jnp.log(n_safe / max_exact) / math.log(max_distance / max_exact) * (num_buckets - max_exact)).astype(jnp.int32)
            val_if_large = jnp.minimum(val_if_large, num_buckets - 1)
            return jnp.where(is_small, n, val_if_large)
        B, T, C = x.shape
        H = N_HEADS
        D = C // H

        def heads(y):
            return y.reshape(B, T, H, D).transpose(0, 2, 1, 3)
        q = heads(x @ Wq + bq)
        k = heads(x @ Wk + bk)
        v = heads(x @ Wv + bv)
        freqs = rotary_freqs(T, D)
        cos, sin = (jnp.cos(freqs), jnp.sin(freqs))
        q = q * cos + rotate_half(q) * sin
        k = k * cos + rotate_half(k) * sin
        pos = jnp.arange(T)
        rel_pos = pos[None, :] - pos[:, None]
        bucket = rel_pos_bucket_causal(rel_pos)
        bias = rel_bias_table[bucket]
        bias = bias.transpose(2, 0, 1)
        att = jnp.einsum('bhid,bhjd->bhij', q, k) + bias[None]
        att = att * (1.0 / math.sqrt(D))
        causal = pos[None, :] <= pos[:, None]
        att = jnp.where(causal[None, None], att, -jnp.inf)
        att = jax.nn.softmax(att, axis=-1)
        y = jnp.einsum('bhij,bhjd->bhid', att, v)
        y = y.transpose(0, 2, 1, 3).reshape(B, T, C)
        return y @ Wp + bp

    def _L0_ffn_ref(x, col_emb, gate_w1, gate_b1, gate_w2, gate_b2, W_cols, b_cols, proj_w, proj_b, ln_g, ln_b):
        import jax, jax.numpy as jnp
        import numpy as np
        NUM_COLUMNS = 16
        INPUT_DIM = 256
        NUM_NEURONS = 64
        SPARSITY = 0.05
        B, S = (4, 512)

        def _l2norm(v, axis=-1, eps=1e-12):
            n = jnp.sqrt(jnp.sum(v * v, axis=axis, keepdims=True))
            return v / jnp.maximum(n, eps)
        Bq, Sq, D = x.shape
        C = col_emb.shape[0]
        similarity = jnp.einsum('bsd,cd->bsc', _l2norm(x), _l2norm(col_emb))
        h = jax.nn.gelu(x @ gate_w1 + gate_b1, approximate=False)
        gate_values = jax.nn.sigmoid(h @ gate_w2 + gate_b2)
        logits = similarity + gate_values
        k = max(1, int(C * SPARSITY))
        _, top_idx = jax.lax.top_k(logits, k)
        mask = jnp.sum(jax.nn.one_hot(top_idx, C, dtype=logits.dtype), axis=-2)
        weights = mask * jax.nn.softmax(logits, axis=-1)
        cols = jax.nn.gelu(jnp.einsum('bsd,cdn->bscn', x, W_cols) + b_cols, approximate=False)
        cols = cols * weights[..., None]
        combined = cols.reshape(Bq, Sq, -1)
        y = combined @ proj_w + proj_b + x
        mu = jnp.mean(y, axis=-1, keepdims=True)
        var = jnp.mean((y - mu) ** 2, axis=-1, keepdims=True)
        out = (y - mu) * jax.lax.rsqrt(var + 1e-05) * ln_g + ln_b
        return out
    x = L0_attn_x
    xn = _layernorm(x, axis=-1)
    x = x + _L0_attn_ref(xn, L0_attn_Wq, L0_attn_bq, L0_attn_Wk, L0_attn_bk, L0_attn_Wv, L0_attn_bv, L0_attn_Wp, L0_attn_bp, L0_attn_rel_bias_table) + _L0_ffn_ref(xn, L0_ffn_col_emb, L0_ffn_gate_w1, L0_ffn_gate_b1, L0_ffn_gate_w2, L0_ffn_gate_b2, L0_ffn_W_cols, L0_ffn_b_cols, L0_ffn_proj_w, L0_ffn_proj_b, L0_ffn_ln_g, L0_ffn_ln_b)
    return x

_drawn_inputs = setup_inputs


def setup_inputs(seed=0):
    import zlib

    import numpy as np

    out = dict(_drawn_inputs(seed))
    spreads = {'L0_attn_bq': (0.0, 0.8),
     'L0_attn_bk': (0.0, 0.8),
     'L0_attn_bv': (0.0, 0.503),
     'L0_attn_bp': (0.0, 0.1),
     'L0_ffn_gate_b1': (0.0, 0.8),
     'L0_ffn_gate_b2': (0.0, 0.8),
     'L0_ffn_b_cols': (0.0, 2.0),
     'L0_ffn_proj_b': (0.0, 0.354),
     'L0_ffn_ln_g': (1.0, 0.2),
     'L0_ffn_ln_b': (0.0, 0.1)}
    factors = {'L0_attn_Wq': 8.0,
     'L0_attn_Wk': 8.0,
     'L0_attn_Wv': 8.0,
     'L0_attn_Wp': 3.412,
     'L0_attn_rel_bias_table': 55.95,
     'L0_ffn_col_emb': 8.0,
     'L0_ffn_gate_w1': 8.0,
     'L0_ffn_gate_w2': 8.0,
     'L0_ffn_W_cols': 8.0,
     'L0_ffn_proj_w': 8.0}
    for name, (base, spread) in spreads.items():
        noise = np.random.default_rng([zlib.crc32(name.encode()), seed]).standard_normal(out[name].shape)
        drawn = base * np.exp(spread * noise) if base else spread * noise
        out[name] = jnp.asarray(drawn.astype(out[name].dtype))
    for name, factor in factors.items():
        out[name] = (out[name] * factor).astype(out[name].dtype)
    return out
```

```python
from contextlib import ExitStack

import numpy as np

import concourse.bass as bass
from concourse import mybir
from concourse.alu_op_type import AluOpType as ALU

F32 = mybir.dt.float32
BF16 = mybir.dt.bfloat16
ACT = mybir.ActivationFunctionType
AX = mybir.AxisListType

P = 128
B, T, C = 8, 1024, 256
H, D = 16, 16
GH = 4
NG = H // GH
NT = T // P
CT = 2
CH = CT * P
NC = T // CH
KC = C // P
E = 16
N = 64
EM = E * N // P
BUCKETS = 32
LOWEST = -3.0e38
OFF = -1.0e30
STACK = 6 * D
Q_PARTS = (0, 0, 1, 1, 0, 2)
K_PARTS = (0, 1, 0, 1, 2, 0)
LEAD = NG + 1
HALF = 512
EXTRA = E
QKV = 3 * C + EXTRA

STEPS = [
    (0, [(0, 0, 0), (1, 128, 512)], 896),
    (0, [(2, 256, 0), (3, 384, 256)], 384),
    (1, [(0, 512, 0), (1, 512, 512)], 1024),
    (1, [(2, 512, 0), (3, 512, 512)], 1024),
    (1, [(4, 512, 0), (5, 640, 512)], 896),
    (1, [(6, 768, 0), (7, 896, 256)], 384),
]
SLOTS = len(STEPS) * GH
BIASED = [0, 1, 3, 4, 5]

ROWS = [(qb, part) for qb in range(NT) for part in range(1 if qb < 4 else 2)]
ROWS_PER_SLOT = 4
ROWS_FROM = 6
SHEAR = 3 * P
N_OFF = 512
CHOSEN_STEPS = 8
NORM_STEPS = 6

FRONT_AT = {0: [("stats", None)], 1: [("center", None)], 2: [("x_turn", None)], 3: [("qk", 0)],
            4: [("v", 0)], 5: [("qk", 1)], 6: [("v", 1)], 7: [("hidden", None)],
            8: [("gate", None)], 9: [("choose", None)], 10: [("qk_turn", 0)],
            11: [("mask_turn", None), ("middle", 0)], 12: [("qk_turn", 1)], 13: [("middle", 1)]}
FINISH_AT = 1
BANKED = {"x_turn", "qk", "v", "hidden", "gate", "qk_turn", "mask_turn", "o_turn", "shift_turn",
          "columns", "y_turn", "project"}
RINGED = {"score", "neurons"}


class Order:

    def __init__(self):
        self.stages, self.banks, self.rings, self.turned = [], 0, 0, {}

    def add(self, stage, g, arg=None):
        if stage == "qk_turn":
            self.turned[arg] = self.banks
        if stage == "middle":
            arg = (arg, self.turned[arg])
        self.stages.append((stage, g, arg, self.banks, self.rings))
        self.banks += stage in BANKED
        self.rings += stage in RINGED


def iteration(batch):
    o = Order()
    for g in range(NG):
        has_front = batch + (g + LEAD) // NC < B
        has_finish = batch + (g + LEAD - 1) // NC < B
        has_next = not (batch == B - 1 and g == NG - 1)
        rows = [(h, k) for h in range(GH) for k in range(len(ROWS))] if has_next else []
        if has_next:
            o.add("load", g)
        for i in range(SLOTS):
            s, h = divmod(i, GH)
            o.add("score", g, (s, h))
            if i % GH == 1 and s >= 1:
                o.add("pv", g, (s - 1, o.rings - 2))
                if s - 1 == 1:
                    o.add("o_out", g, 0)
            if i >= ROWS_FROM:
                for _ in range(min(ROWS_PER_SLOT, len(rows))):
                    o.add("row", g, rows.pop(0))
            if i == FINISH_AT and has_finish:
                o.add("finish", g)
            if has_front:
                for stage, arg in FRONT_AT.get(i, ()):
                    o.add(stage, g, arg)
            if i == 14:
                o.add("o_turn", g, 0)
            if has_next and i == 18:
                o.add("shift", g)
            if has_next and i == 19:
                o.add("shift_turn", g)
        o.add("pv", g, (len(STEPS) - 1, o.rings))
        o.add("o_out", g, 1)
        if has_front:
            o.add("neurons", g, 0)
            o.add("neurons", g, 1)
        o.add("o_turn", g, 1)
        if has_front:
            o.add("columns", g)
    for k in range(NC):
        o.add("y_turn", NG - 1, k)
        o.add("project", NG - 1, k)
    return o


def prologue():
    o = Order()
    for g in range(-LEAD, 0):
        for i in sorted(FRONT_AT):
            if i == FINISH_AT and g > -LEAD:
                o.add("finish", g)
            for stage, arg in FRONT_AT[i]:
                o.add(stage, g, arg)
        o.add("neurons", g, 0)
        o.add("neurons", g, 1)
        o.add("columns", g)
    o.add("load", -1)
    for h in range(GH):
        for k in range(len(ROWS)):
            o.add("row", -1, (h, k))
    o.add("shift", -1)
    o.add("shift_turn", -1)
    return o


def layer_kernel(nc, a, out):
    ctx = ExitStack()
    with ctx:
        def sb(name, shape, dt=F32):
            return ctx.enter_context(nc.sbuf_tensor(name, shape, dt))

        def pb(name, shape, dt=F32):
            return ctx.enter_context(nc.psum_tensor(name, shape, dt))

        def sem(name):
            return ctx.enter_context(nc.semaphore(name))

        parts_d = nc.dram_tensor("parts_d", (B, 3, 2 * KC, P, T), BF16, kind="Internal").ap()
        v_d = nc.dram_tensor("v_d", (B, P, NT, C), F32, kind="Internal").ap()
        rest_d = nc.dram_tensor("rest_d", (B, P, NT, C), F32, kind="Internal").ap()
        offsets_d = nc.dram_tensor("offsets_d", (2, H, N_OFF), F32, kind="Internal").ap()
        sheared_d = nc.dram_tensor("sheared_d", (2, H, P, SHEAR), F32, kind="Internal").ap()

        ident = sb("ident", [P, P])
        ident_b = sb("ident_b", [P, P], BF16)
        w_qkv = sb("w_qkv", [P, KC, QKV])
        w_out = sb("w_out", [P, KC, C])
        w_hid = sb("w_hid", [P, KC, P])
        w_gate = sb("w_gate", [P, E])
        w_cols = sb("w_cols", [P, KC, E * N])
        w_proj = sb("w_proj", [P, EM, C])
        b_qkv = sb("b_qkv", [P, 3 * C])
        b_gate = sb("b_gate", [P, E])
        b_hid = sb("b_hid", [P, 1])
        b_cols = sb("b_cols", [P, EM])
        b_proj = sb("b_proj", [P, C])
        gain = sb("gain", [P, C])
        b_rest = sb("b_rest", [P, C])
        rank = sb("rank", [P, E])
        power = sb("power", [P, CT])
        rotary = sb("rotary", [P, NT, 3, D // 2])
        pick = sb("pick", [E, EM * P], BF16)
        near_rows = sb("near_rows", [P, H, 2 * P])
        near_cols = sb("near_cols", [P, H, 2 * P])

        x = sb("x", [P, 2, CT, C])
        stats = sb("stats", [P, CT, 6])
        moments = sb("moments", [P, CT, 2])
        rstd = sb("rstd", [P, CT])
        norm = sb("norm", [P, 6, CT])
        xn = sb("xn", [P, CT, C])
        xn_t = sb("xn_t", [P, KC, CH])
        skip = sb("skip", [P, CT, C])
        rest = sb("rest", [P, CT, C])
        qk = sb("qk", [P, CT, 2 * C])
        swapped = sb("swapped", [P, 2 * C])
        rot = sb("rot", [P, CT, 2 * C])
        parts = [sb(f"part{i}", [P, 2 * KC, CH], BF16) for i in range(3)]
        left = sb("left", [P, 2 * KC, P])
        v = sb("v", [P, CT, C])
        like = sb("like", [P, CT, E])
        hid_t = sb("hid_t", [P, CH])
        gate_in = sb("gate_in", [P, CT, E])
        gate_th = sb("gate_th", [P, CT, E])
        logits = sb("logits", [P, CT, E])
        top = sb("top", [P, CT])
        tied = sb("tied", [P, CT, E])
        ranked = sb("ranked", [P, CT, E])
        first = sb("first", [P, CT])
        others = sb("others", [P, CT, E])
        below = sb("below", [P, CT, E])
        shares = sb("shares", [P, CT, E])
        total = sb("total", [P, CT])
        weight = sb("weight", [P, CT])
        others_t = sb("others_t", [E, CH], BF16)
        act_t = sb("act_t", [P, EM, CH])
        y2 = sb("y2", [P, CT, C])
        stats2 = sb("stats2", [P, CT, 6])
        moments2 = sb("moments2", [P, CT, 2])
        rstd2 = sb("rstd2", [P, CT])
        y2n = sb("y2n", [P, CT, C])

        stack_q = [sb(f"stack_q{i}", [STACK + 3, GH, T], BF16) for i in range(2)]
        stack_k = [sb(f"stack_k{i}", [STACK + 3, GH, T], BF16) for i in range(2)]
        v_in = sb("v_in", [P, NT, GH * D])
        v_aug = [sb(f"v_aug{i}", [P, NT, GH, 32]) for i in range(2)]
        maxima = sb("maxima", [P, 3, GH * NT])
        shift = sb("shift", [P, GH * NT])
        shift_l = sb("shift_l", [P, 2, GH * NT])
        shift_p = sb("shift_p", [P, 3, GH * NT], BF16)
        shift_t = sb("shift_t", [3 * GH * NT, P], BF16)
        probs = sb("probs", [P, 2, GH, 1024])
        o_sb = sb("o_sb", [P, HALF])
        inv = sb("inv", [P, 4, GH])
        y = sb("y", [P, NT, C])
        y_t = sb("y_t", [P, KC, CH])
        result = sb("result", [P, 2, CT, C])

        ring = [pb(f"scores{i}", [P, 1024]) for i in range(2)]
        row_ring = [pb(f"rows{i}", [P, 512]) for i in range(2)]
        o_bank = pb("o_bank", [P, HALF])
        bank = pb("bank", [P, 512])

        weights_in = sem("weights_in")
        columns_in = sem("columns_in")
        filled = sem("filled")
        embedded = sem("embedded")
        rest_bias = sem("rest_bias")
        cast = sem("cast")
        offsets_made = sem("offsets_made")
        offsets_out = sem("offsets_out")
        sheared = sem("sheared")
        near_in = sem("near_in")
        x_in = [sem(f"x_in{i}") for i in range(2)]
        bank_filled = sem("bank_filled")
        bank_drained = sem("bank_drained")
        ring_filled = sem("ring_filled")
        ring_biased = sem("ring_biased")
        ring_drained = sem("ring_drained")
        rows_filled = sem("rows_filled")
        rows_drained = sem("rows_drained")
        stats_done = sem("stats_done")
        moments_ready = sem("moments_ready")
        rstd_ready = sem("rstd_ready")
        norm_step = sem("norm_step")
        xn_ready = sem("xn_ready")
        skip_ready = sem("skip_ready")
        rest_ready = sem("rest_ready")
        rope_step = sem("rope_step")
        rot_ready = sem("rot_ready")
        v_ready = sem("v_ready")
        hi_ready = sem("hi_ready")
        mid_ready = sem("mid_ready")
        lo_ready = sem("lo_ready")
        parts_out = [sem(f"parts_out{i}") for i in range(3)]
        v_out = sem("v_out")
        rest_out = sem("rest_out")
        tanh_ready = sem("tanh_ready")
        chosen = sem("chosen")
        share_ready = sem("share_ready")
        weight_ready = sem("weight_ready")
        stats2_done = sem("stats2_done")
        moments2_ready = sem("moments2_ready")
        rstd2_ready = sem("rstd2_ready")
        y2n_ready = sem("y2n_ready")
        scaled = sem("scaled")
        rest_all = sem("rest_all")
        stack_in = [sem(f"stack_in{i}") for i in range(2)]
        v_in_done = sem("v_in_done")
        v_aug_ready = sem("v_aug_ready")
        shift_step = sem("shift_step")
        counted = sem("counted")
        shift_in = sem("shift_in")
        probs_used = sem("probs_used")
        o_out = sem("o_out")
        inv_ready = sem("inv_ready")
        rest_in_done = [sem(f"rest_in{i}") for i in range(2)]
        result_out = [sem(f"result_out{i}") for i in range(2)]

        LOOPS = B - 2
        pro, body_, last2, last = prologue(), iteration(0), iteration(B - 2), iteration(B - 1)
        assert pro.rings % 2 == 0 and body_.rings % 2 == 0 and last2.rings % 2 == 0
        SETUP = 4
        bank0 = SETUP + pro.banks

        def run(engine, body):
            body(pro.stages, -1, SETUP, 0)
            with engine.Fori(0, LOOPS) as b:
                body(body_.stages, b, b * body_.banks + bank0, b * body_.rings + pro.rings)
            bank6, ring6 = bank0 + LOOPS * body_.banks, pro.rings + LOOPS * body_.rings
            body(last2.stages, B - 2, bank6, ring6)
            body(last.stages, B - 1, bank6 + last2.banks, ring6 + last2.rings)

        def chunk_of(b, g):
            n = g + LEAD
            if g < 0:
                return n // NC, n % NC, n
            fb, c = b + n // NC, n % NC
            return fb, c, fb * NC + c

        def next_group(b, g):
            ab, ag = (0, 0) if g < 0 else (b, g + 1) if g + 1 < NG else (b + 1, 0)
            return ab, ag, ab * NG + ag

        def wait(eng, s, value):
            if not isinstance(value, int) or value > 0:
                eng.wait_ge(s, value)

        def alone(eng):
            eng.sem_inc(counted, 1)

        block = ctx.enter_context(nc.Block())

        @block.sync
        def _(sp):
            def every(ap1d, n):
                return bass.AP(ap1d.tensor, 0, [[0, P], [1, n]])

            first_in = [
                (ident[:, :], a["ident"]), (rank[:, :], every(a["rank"], E)),
                (rotary[:, :, :, :], a["rotary"]),
                (w_qkv[:, :, 0:C], a["Wq"].rearrange("(k p) n -> p k n", p=P)),
                (w_qkv[:, :, C:2 * C], a["Wk"].rearrange("(k p) n -> p k n", p=P)),
                (w_qkv[:, :, 2 * C:3 * C], a["Wv"].rearrange("(k p) n -> p k n", p=P)),
                (b_qkv[:, 0:C], every(a["bq"], C)), (b_qkv[:, C:2 * C], every(a["bk"], C)),
                (b_qkv[:, 2 * C:3 * C], every(a["bv"], C)),
                (w_hid[:, :, :], a["gate_w1"].rearrange("(k p) n -> p k n", p=P)),
                (b_hid[:, :], a["gate_b1"].rearrange("(p o) -> p o", o=1)),
                (w_gate[:, :], a["gate_w2"]), (b_gate[:, :], every(a["gate_b2"], E)),
                (b_proj[:, :], every(a["proj_b"], C)), (gain[:, :], every(a["ln_g"], C)),
                (b_rest[:, :], every(a["bp"], C)), (skip[:, 0, :], every(a["ln_b"], C)),
                (w_out[:, :, :], a["Wp"].rearrange("(k p) n -> p k n", p=P)),
                (w_proj[:, :, :], a["proj_w"].rearrange("(m p) n -> p m n", p=P)),
                (act_t[0:E, 0, :], a["col_emb"]),
                (act_t[0:E, 1:5, :].rearrange("p m n -> p (m n)"), a["pick"]),
                (y2[0:BUCKETS, 0, 0:H], a["rel_bias_table"]),
                (qk[0:BUCKETS + 1, :, :], a["offset_picks"])]
            assert len(first_in) == LOADS
            with nc.allow_non_contiguous_dma(reason="one bias per partition, once"):
                for dst, src in first_in:
                    sp.dma_start(dst, src).then_inc(weights_in, 16)
                for k in range(KC):
                    sp.dma_start(w_cols[:, k, :].rearrange("p (c n) -> p c n", n=N),
                                 a["W_cols"][:, k * P:(k + 1) * P, :].rearrange("c p n -> p c n")) \
                        .then_inc(columns_in, 16)
                sp.dma_start(b_cols[:, :], bass.AP(a["b_cols"].tensor, 0, [[1, P], [P, EM]])) \
                    .then_inc(columns_in, 16)
            sp.sem_inc(result_out[0], 16)
            sp.sem_inc(result_out[1], 16)
            sp.wait_ge(offsets_made, 2)
            sp.dma_start(offsets_d.rearrange("r h n -> h r n"), rot[0:H, :, :]).then_inc(offsets_out, 16)
            sp.wait_ge(offsets_out, 16)
            for r in range(2):
                sp.dma_start(sheared_d[r], bass.AP(offsets_d.tensor, r * (H * N_OFF + P),
                                                   [[N_OFF, H], [0, P], [1, SHEAR]])).then_inc(sheared, 16)
            sp.wait_ge(sheared, 32)
            for r, near in enumerate((near_cols, near_rows)):
                sp.dma_start(near[:, :, :], bass.AP(sheared_d.tensor, r * H * P * SHEAR + P - r,
                                                    [[SHEAR - 1, P], [P * SHEAR, H], [1, 2 * P]])) \
                    .then_inc(near_in, 16)

            x_v = a["x"].rearrange("b (c t p) f -> b c p t f", c=NC, p=P)
            out_v = out.rearrange("b (c t p) f -> b c p t f", c=NC, p=P)

            def load_x(fb, c):
                wait(sp, xn_ready, fb * NC + c - 1)
                wait(sp, rest_ready, fb * NC + c - 1)
                alone(sp)
                sp.dma_start(x[:, c % 2], x_v[fb, c]).then_inc(x_in[c % 2], 16)

            def store_rest(fb, c, n):
                mb, mc = (fb, c - 1) if c else (fb - 1, NC - 1)
                sp.wait_ge(rest_all, n)
                alone(sp)
                sp.dma_start(rest_d[mb, :, mc * CT:(mc + 1) * CT, :], rest[:, :, :]).then_inc(rest_out, 16)

            def body(stages, b, bank_n, ring_n):
                if isinstance(b, int) and b < 0:
                    load_x(0, 0)
                    load_x(0, 1)
                for stage, g, arg, banks, rings in stages:
                    fb, c, n = chunk_of(b, g)
                    ab, ag, gi = next_group(b, g)
                    if stage == "load":
                        for i in range(3):
                            sp.wait_ge(parts_out[i], (ab + 1) * (NC * 16))
                        sp.wait_ge(v_out, (ab + 1) * (NC * 16))
                        alone(sp)
                        if g >= 0:
                            sp.wait_ge(ring_filled, ring_n + rings)
                        alone(sp)
                        half = slice((ag % 2) * GH * D, (ag % 2 + 1) * GH * D)
                        for r in range(6):
                            for stk, side, which in ((stack_q, 0, Q_PARTS), (stack_k, KC, K_PARTS)):
                                src = parts_d[ab, which[r], side + ag // 2, half, :]
                                sp.dma_start(stk[ag % 2][r * D:(r + 1) * D],
                                             src.rearrange("(h d) t -> d h t", d=D)) \
                                    .then_inc(stack_in[ag % 2], 16)
                        wait(sp, v_aug_ready, gi)
                        alone(sp)
                        sp.dma_start(v_in[:, :, :], v_d[ab, :, :, ag * GH * D:(ag + 1) * GH * D]) \
                            .then_inc(v_in_done, 16)
                    elif stage == "v" and arg == 1:
                        sp.wait_ge(v_ready, n * CT + CT)
                        alone(sp)
                        sp.dma_start(v_d[fb, :, c * CT:(c + 1) * CT, :], v[:, :, :]).then_inc(v_out, 16)
                        if g > -LEAD:
                            store_rest(fb, c, n)
                    elif stage == "mask_turn":
                        if not isinstance(n, int) or n + 2 < B * NC:
                            load_x(*((fb, c + 2) if c + 2 < NC else (fb + 1, c + 2 - NC)))
                    elif stage == "middle" and arg[0] == 1:
                        for i, ready in enumerate((hi_ready, mid_ready, lo_ready)):
                            sp.wait_ge(ready, n * CT + CT)
                            alone(sp)
                            sp.dma_start(parts_d[fb, i, :, :, c * CH:(c + 1) * CH].rearrange("q p t -> p q t"),
                                         parts[i][:, :, :]).then_inc(parts_out[i], 16)
                    elif stage == "finish" and isinstance(n, int) and n == B * NC:
                        store_rest(fb, c, n)
                    elif stage == "shift_turn":
                        sp.wait_ge(bank_drained, bank_n + (banks + 2))
                        sp.dma_start(stack_q[ag % 2][STACK:STACK + 3].rearrange("r h (q t) -> r (h q) t", t=P),
                                     shift_t[:, :]).then_inc(shift_in, 16)
                    elif stage == "y_turn" and arg == 0:
                        sp.wait_ge(rest_out, (b + 1) * (NC * 16))
                        for k in range(2):
                            sp.wait_ge(result_out[k], b * (NC // 2 * 16) + 16)
                            alone(sp)
                            sp.dma_start(result[:, k], rest_d[b, :, k * CT:(k + 1) * CT, :]) \
                                .then_inc(rest_in_done[k], 16)
                    elif stage == "project":
                        sp.wait_ge(bank_drained, bank_n + (banks + 2))
                        alone(sp)
                        sp.dma_start(out_v[b, arg], result[:, arg % 2]).then_inc(result_out[arg % 2], 16)
                        k = arg + 1
                        if 2 <= k < NC:
                            sp.wait_ge(result_out[k % 2], b * (NC // 2 * 16) + (k // 2 + 1) * 16)
                            alone(sp)
                            sp.dma_start(result[:, k % 2], rest_d[b, :, k * CT:(k + 1) * CT, :]) \
                                .then_inc(rest_in_done[k % 2], 16)

            run(sp, body)
            for i in range(2):
                sp.wait_ge(result_out[i], 16 + B * NC // 2 * 16)
                sp.wait_ge(parts_out[i], B * NC * 16)
            sp.wait_ge(parts_out[2], B * NC * 16)
            sp.wait_ge(v_out, B * NC * 16)
            sp.wait_ge(rest_out, B * NC * 16)

        @block.gpsimd
        def _(pool):
            fills = [(power[:, :], -0.5), (maxima[:, :, :], LOWEST),
                     (y2[BUCKETS:BUCKETS + 1, 0, 0:H], LOWEST)]
            for i in range(2):
                fills += [(v_aug[i][:, :, :, :], 0.0), (v_aug[i][:, :, :, D:D + 1], 1.0),
                          (stack_k[i][STACK:STACK + 3], 1.0)]
            assert len(fills) == FILLS
            for k, (dst, value) in enumerate(fills):
                wait(pool, filled, k)
                pool.memset(dst, value).then_inc(filled, 1)
            pool.wait_ge(embedded, 1)
            pool.tensor_scalar(norm[0:E, 1, 0:1], norm[0:E, 0, 0:1], 1e-24, None, ALU.max).then_inc(embedded, 1)
            pool.wait_ge(embedded, 2)
            pool.tensor_tensor(norm[0:E, 2, 0:1], norm[0:E, 1, 0:1], power[0:E, 0:1], ALU.pow) \
                .then_inc(embedded, 1)
            pool.wait_ge(weights_in, LOADS * 16)
            pool.tensor_tensor(b_rest[:, :], b_rest[:, :], skip[:, 0, :], ALU.add).then_inc(rest_bias, 1)
            pool.wait_ge(rest_bias, 1)
            pool.wait_ge(embedded, 4)

            def body(stages, b, bank_n, ring_n):
                for stage, g, arg, banks, rings in stages:
                    fb, c, n = chunk_of(b, g)
                    ab, ag, gi = next_group(b, g)
                    if stage == "stats":
                        wait(pool, rstd_ready, n)
                        pool.wait_ge(moments_ready, n + 1)
                        alone(pool)
                        pool.tensor_scalar(norm[:, 0, :], moments[:, :, 1], 1e-5, None, ALU.add) \
                            .then_inc(norm_step, 1)
                        pool.wait_ge(norm_step, n * NORM_STEPS + 1)
                        pool.tensor_tensor(rstd[:, :], norm[:, 0, :], power[:, :], ALU.pow) \
                            .then_inc(rstd_ready, 1)
                    elif stage == "finish":
                        pool.wait_ge(y2n_ready, n)
                        for t in range(CT):
                            ins = pool.tensor_tensor(y2n[:, t, :], y2n[:, t, :], gain[:, :], ALU.mult)
                        ins.then_inc(scaled, 1)
                        pool.wait_ge(scaled, n)
                        pool.tensor_tensor(rest[:, :, :], rest[:, :, :], y2n[:, :, :], ALU.add) \
                            .then_inc(rest_all, 1)
                    elif stage == "x_turn":
                        pool.wait_ge(rstd_ready, n + 1)
                        pool.wait_ge(norm_step, n * NORM_STEPS + 1)
                        pool.tensor_tensor(norm[:, 1, :], rstd[:, :], rstd[:, :], ALU.mult).then_inc(norm_step, 1)
                        pool.wait_ge(norm_step, n * NORM_STEPS + 2)
                        pool.tensor_tensor(norm[:, 2, :], norm[:, 1, :], moments[:, :, 1], ALU.mult) \
                            .then_inc(norm_step, 1)
                        pool.wait_ge(norm_step, n * NORM_STEPS + 3)
                        alone(pool)
                        pool.tensor_scalar(norm[:, 3, :], norm[:, 2, :], float(C), 1e-24, ALU.mult, ALU.max) \
                            .then_inc(norm_step, 1)
                        pool.wait_ge(norm_step, n * NORM_STEPS + 4)
                        pool.tensor_tensor(norm[:, 4, :], norm[:, 3, :], power[:, :], ALU.pow) \
                            .then_inc(norm_step, 1)
                        pool.wait_ge(xn_ready, n + 1)
                        for t in range(CT):
                            ins = pool.tensor_tensor(skip[:, t, :], xn[:, t, :], b_proj[:, :], ALU.add)
                        ins.then_inc(skip_ready, 1)
                    elif stage == "qk":
                        t = arg
                        q4 = qk[:, t, :].rearrange("p (h s e) -> p h s e", s=2, e=D // 2)
                        s4 = swapped[:, :].rearrange("p (h s e) -> p h s e", s=2, e=D // 2)

                        def table(k, halves):
                            return rotary[:, c * CT + t, k, :].rearrange("p (h s e) -> p h s e", h=1, s=1) \
                                .to_broadcast((P, 2 * H, halves, D // 2))
                        r4 = rot[:, t, :].rearrange("p (h s e) -> p h s e", s=2, e=D // 2)
                        pool.wait_ge(bank_drained, bank_n + (banks + 2))
                        wait(pool, rot_ready, n * CT + t)
                        pool.tensor_tensor(s4[:, :, 0:1, :], q4[:, :, 1:2, :], table(2, 1), ALU.mult)
                        pool.tensor_tensor(s4[:, :, 1:2, :], q4[:, :, 0:1, :], table(1, 1), ALU.mult)
                        wait(pool, hi_ready, n * CT + (t + 1 - CT))
                        pool.tensor_tensor(r4, q4, table(0, 2), ALU.mult).then_inc(rope_step, 1)
                        pool.wait_ge(rope_step, n * CT + (t + 1))
                        pool.tensor_tensor(rot[:, t, :], rot[:, t, :], swapped[:, :], ALU.add).then_inc(rot_ready, 1)
                    elif stage == "mask_turn":
                        wait(pool, rest_out, n * 16)
                        for t in range(CT):
                            ins = pool.tensor_tensor(rest[:, t, :], x[:, c % 2, t, :], b_rest[:, :], ALU.add)
                        ins.then_inc(rest_ready, 1)
                    elif stage == "middle":
                        t = arg[0]
                        pool.wait_ge(mid_ready, n * CT + (t + 1))
                        wait(pool, parts_out[2], n * 16)
                        pool.tensor_tensor(parts[2][:, :, t * P:(t + 1) * P], left[:, :, :],
                                           parts[1][:, :, t * P:(t + 1) * P], ALU.subtract).then_inc(lo_ready, 1)
                    elif stage == "shift_turn":
                        pool.wait_ge(v_in_done, gi * 16 + 16)
                        wait(pool, probs_used, (gi - 1) * len(STEPS) + 2)
                        alone(pool)
                        pool.tensor_copy(v_aug[ag % 2][:, :, :, 0:D],
                                         v_in[:, :, :].rearrange("p t (h d) -> p t h d", d=D)) \
                            .then_inc(v_aug_ready, 1)
                    elif stage == "columns":
                        wait(pool, rstd2_ready, n)
                        pool.wait_ge(moments2_ready, n + 1)
                        alone(pool)
                        pool.tensor_scalar(norm[:, 5, :], moments2[:, :, 1], 1e-5, None, ALU.add) \
                            .then_inc(norm_step, 1)
                        pool.wait_ge(norm_step, n * NORM_STEPS + 6)
                        pool.tensor_tensor(rstd2[:, :], norm[:, 5, :], power[:, :], ALU.pow) \
                            .then_inc(rstd2_ready, 1)

            run(pool, body)

        @block.scalar
        def _(act):
            act.sem_inc(bank_drained, 1)
            act.sem_inc(ring_drained, 2)
            act.sem_inc(o_out, 1)
            act.wait_ge(weights_in, LOADS * 16)
            act.activation(ident_b[:, :], ident[:, :], ACT.Copy).then_inc(cast, 1)
            act.activation(pick[:, :], act_t[0:E, 1:5, :].rearrange("p m n -> p (m n)"), ACT.Copy) \
                .then_inc(cast, 1)
            for r in range(2):
                act.wait_ge(bank_filled, r + 1)
                act.activation(rot[0:H, r, :], bank[0:H, :], ACT.Copy).then_inc(offsets_made, 1)
                act.wait_ge(offsets_made, r + 1)
                act.sem_inc(bank_drained, 1)
            act.wait_ge(bank_filled, 3)
            act.activation(w_qkv[:, :, 3 * C:QKV], bank[:, 0:KC * E].rearrange("p (k e) -> p k e", e=E),
                           ACT.Copy).then_inc(cast, 1)
            act.wait_ge(cast, 3)
            act.sem_inc(bank_drained, 2)
            act.wait_ge(columns_in, (KC + 1) * 16)
            act.wait_ge(offsets_out, 16)

            def body(stages, b, bank_n, ring_n):
                for stage, g, arg, banks, rings in stages:
                    fb, c, n = chunk_of(b, g)
                    ab, ag, gi = next_group(b, g)
                    if stage == "score":
                        s, h = arg
                        if s in BIASED:
                            act.wait_ge(ring_biased, b * (NG * GH * len(BIASED))
                                        + (g * GH * len(BIASED) + BIASED.index(s) * GH + h + 1))
                        else:
                            act.wait_ge(ring_filled, ring_n + (rings + 1))
                        if h == 0:
                            act.wait_ge(probs_used, b * (NG * len(STEPS)) + (g * len(STEPS) + s + 1))
                        width = STEPS[s][2]
                        act.activation(probs[:, s % 2, h, 0:width], ring[rings % 2][:, 0:width], ACT.Exp,
                                       scale=float(D) ** -0.5).then_inc(ring_drained, 1)
                    elif stage == "o_out":
                        k = b * (2 * NG) + (2 * g + arg)
                        last_step = (1, len(STEPS) - 1)[arg]
                        act.wait_ge(probs_used, b * (NG * len(STEPS)) + (g * len(STEPS) + last_step + 3))
                        act.wait_ge(inv_ready, k + 1)
                        act.activation(o_sb[:, :], o_bank[:, :], ACT.Copy).then_inc(o_out, 1)
                    elif stage == "x_turn":
                        act.wait_ge(bank_filled, bank_n + (banks + 1))
                        for t in range(CT):
                            ins = act.activation(xn_t[:, :, t * P:(t + 1) * P],
                                                 bank[:, t * C:(t + 1) * C].rearrange("p (k n) -> p k n", n=P),
                                                 ACT.Copy)
                        ins.then_inc(bank_drained, 1)
                    elif stage == "hidden":
                        act.wait_ge(bank_filled, bank_n + (banks + 1))
                        act.activation(hid_t[:, :], bank[:, 0:CH], ACT.Gelu, bias=b_hid[:, 0:1]) \
                            .then_inc(bank_drained, 1)
                    elif stage == "gate":
                        act.wait_ge(bank_drained, bank_n + (banks + 2))
                        act.activation(gate_th[:, :, :], gate_in[:, :, :], ACT.Tanh, scale=0.5) \
                            .then_inc(tanh_ready, 1)
                    elif stage == "choose":
                        act.wait_ge(chosen, n * CHOSEN_STEPS + 4)
                        act.activation(shares[:, :, :], below[:, :, :], ACT.Exp).then_inc(share_ready, 1)
                    elif stage == "qk_turn":
                        t = arg
                        act.wait_ge(bank_filled, bank_n + (banks + 1))
                        wait(act, parts_out[0], n * 16)
                        act.activation(parts[0][:, :, t * P:(t + 1) * P],
                                       bank[:, :].rearrange("p (q n) -> p q n", n=P), ACT.Copy) \
                            .then_inc(hi_ready, 1)
                    elif stage == "middle":
                        t, turned = arg
                        act.wait_ge(bank_drained, bank_n + (turned + 2))
                        wait(act, parts_out[1], n * 16)
                        act.activation(parts[1][:, :, t * P:(t + 1) * P], left[:, :, :], ACT.Copy) \
                            .then_inc(mid_ready, 1)
                    elif stage == "mask_turn":
                        act.wait_ge(bank_filled, bank_n + (banks + 1))
                        act.activation(others_t[:, :], bank[0:E, 0:CH], ACT.Copy).then_inc(bank_drained, 1)
                    elif stage == "shift_turn":
                        act.wait_ge(bank_filled, bank_n + (banks + 1))
                        wait(act, shift_in, gi * 16)
                        act.activation(shift_t[:, :], bank[:, :].bitcast(BF16)[0:3 * GH * NT, 0:P], ACT.Copy) \
                            .then_inc(bank_drained, 1)
                    elif stage == "neurons":
                        act.wait_ge(ring_filled, ring_n + (rings + 1))
                        for m in range(EM // 2):
                            mm = arg * (EM // 2) + m
                            ins = act.activation(act_t[:, mm, :], ring[rings % 2][:, m * CH:(m + 1) * CH],
                                                 ACT.Gelu, bias=b_cols[:, mm:mm + 1])
                        ins.then_inc(ring_drained, 1)
                    elif stage == "y_turn":
                        act.wait_ge(bank_filled, bank_n + (banks + 1))
                        for t in range(CT):
                            ins = act.activation(y_t[:, :, t * P:(t + 1) * P],
                                                 bank[:, t * C:(t + 1) * C].rearrange("p (k n) -> p k n", n=P),
                                                 ACT.Copy)
                        ins.then_inc(bank_drained, 1)

            run(act, body)

        @block.tensor
        def _(pe):
            pe.wait_ge(weights_in, LOADS * 16)
            pe.wait_ge(filled, FILLS)
            for r in range(2):
                pe.wait_ge(bank_drained, r + 1)
                pe.matmul(bank[0:H, :], y2[0:BUCKETS + 1, 0, 0:H], qk[0:BUCKETS + 1, r, :],
                          start=True, stop=True).then_inc(bank_filled, 1)
            pe.wait_ge(bank_drained, 3)
            pe.wait_ge(embedded, 4)
            for k in range(KC):
                ins = pe.transpose(bank[:, k * E:(k + 1) * E], y2n[0:E, 1, k * P:(k + 1) * P], ident[0:E, 0:E])
            ins.then_inc(bank_filled, 1)
            pe.wait_ge(bank_drained, 5)
            pe.wait_ge(cast, 3)
            pe.nop().then_inc(bank_filled, 1)
            pe.wait_ge(columns_in, (KC + 1) * 16)
            pe.sem_inc(probs_used, 2)

            def body(stages, b, bank_n, ring_n):
                for stage, g, arg, banks, rings in stages:
                    fb, c, n = chunk_of(b, g)
                    ab, ag, gi = next_group(b, g)
                    G = b * NG + g
                    if stage in BANKED:
                        pe.wait_ge(bank_drained, bank_n + (banks + 1))
                    if stage == "score":
                        s, h = arg
                        pe.wait_ge(ring_drained, ring_n + (rings + 1))
                        if s == 0 and h == 0:
                            pe.wait_ge(shift_in, G * 16 + 16)
                        half, blocks, _ = STEPS[s]
                        for kb, q0, c0 in blocks:
                            w = (half + 1) * HALF - q0
                            ins = pe.matmul(ring[rings % 2][:, c0:c0 + w],
                                            stack_k[g % 2][:, h, kb * P:(kb + 1) * P],
                                            stack_q[g % 2][:, h, q0:q0 + w], start=True, stop=True)
                        ins.then_inc(ring_filled, 1)
                    elif stage == "pv":
                        s, rings_done = arg
                        half, blocks, _ = STEPS[s]
                        if s == 0:
                            pe.wait_ge(v_aug_ready, G + 1)
                        if s in (0, 2):
                            pe.wait_ge(o_out, b * (2 * NG) + (2 * g + half + 1))
                        pe.wait_ge(ring_drained, ring_n + (rings_done + 2))
                        for kb, q0, c0 in blocks:
                            w = (half + 1) * HALF - q0
                            for h in range(GH):
                                ins = pe.matmul(o_bank[32 * h:32 * h + 32, HALF - w:HALF],
                                                v_aug[g % 2][:, kb, h, :], probs[:, s % 2, h, c0:c0 + w],
                                                start=(kb == 0), stop=(kb == 4 * half + 3))
                        ins.then_inc(probs_used, 1)
                    elif stage == "row":
                        h, k = arg
                        qb, part = ROWS[k]
                        i = gi * (GH * len(ROWS)) + (h * len(ROWS) + k)
                        if h == 0 and k == 0:
                            pe.wait_ge(stack_in[ag % 2], (ab * (NG // 2) + (ag // 2 + 1)) * (12 * 16))
                        pe.wait_ge(rows_drained, i + 1)
                        tile = row_ring[(h * len(ROWS) + k) % 2]
                        q = stack_q[ag % 2][0:STACK, h, qb * P:(qb + 1) * P]
                        keys = stack_k[ag % 2][0:STACK, h, :]
                        far = max(qb - 1, 0) * P
                        if part == 0:
                            ins = pe.matmul(tile[:, 0:(qb + 1) * P - far], q, keys[:, far:(qb + 1) * P],
                                            start=True, stop=True)
                            if far:
                                w = min(far, 2 * P)
                                ins = pe.matmul(tile[:, 2 * P:2 * P + w], q, keys[:, 0:w], start=True, stop=True)
                        else:
                            ins = pe.matmul(tile[:, 0:far - 2 * P], q, keys[:, 2 * P:far], start=True, stop=True)
                        ins.then_inc(rows_filled, 1)
                    elif stage == "x_turn":
                        pe.wait_ge(xn_ready, n + 1)
                        for t in range(CT):
                            for k in range(KC):
                                ins = pe.transpose(bank[:, (t * KC + k) * P:(t * KC + k + 1) * P],
                                                   xn[:, t, k * P:(k + 1) * P], ident[:, :])
                        ins.then_inc(bank_filled, 1)
                    elif stage in ("qk", "v"):
                        cols = slice(0, 2 * C) if stage == "qk" else slice(2 * C, QKV)
                        for k in range(KC):
                            ins = pe.matmul(bank[:, 0:cols.stop - cols.start],
                                            xn_t[:, k, arg * P:(arg + 1) * P], w_qkv[:, k, cols],
                                            start=(k == 0), stop=(k == KC - 1))
                        ins.then_inc(bank_filled, 1)
                    elif stage == "hidden":
                        for k in range(KC):
                            ins = pe.matmul(bank[:, 0:CH], w_hid[:, k, :], xn_t[:, k, :],
                                            start=(k == 0), stop=(k == KC - 1))
                        ins.then_inc(bank_filled, 1)
                    elif stage == "gate":
                        for t in range(CT):
                            ins = pe.matmul(bank[:, t * E:(t + 1) * E], hid_t[:, t * P:(t + 1) * P],
                                            w_gate[:, :], start=True, stop=True)
                        ins.then_inc(bank_filled, 1)
                    elif stage == "qk_turn":
                        pe.wait_ge(rot_ready, n * CT + (arg + 1))
                        for q in range(2 * KC):
                            ins = pe.transpose(bank[:, q * P:(q + 1) * P], rot[:, arg, q * P:(q + 1) * P],
                                               ident[:, :])
                        ins.then_inc(bank_filled, 1)
                    elif stage == "mask_turn":
                        pe.wait_ge(chosen, n * CHOSEN_STEPS + 7)
                        for t in range(CT):
                            ins = pe.transpose(bank[0:E, t * P:(t + 1) * P], others[:, t, :], ident[:, :])
                        ins.then_inc(bank_filled, 1)
                    elif stage == "shift_turn":
                        pe.wait_ge(shift_step, gi * 6 + 6)
                        pe.transpose(bank[:, :].bitcast(BF16)[0:3 * GH * NT, 0:P],
                                     shift_p[:, :, :].rearrange("p r j -> p (r j)"), ident_b[:, :]) \
                            .then_inc(bank_filled, 1)
                    elif stage == "neurons":
                        pe.wait_ge(ring_drained, ring_n + (rings + 1))
                        pe.wait_ge(bank_drained, bank_n + (banks + 1))
                        for m in range(EM // 2):
                            mm = arg * (EM // 2) + m
                            dst = ring[rings % 2][:, m * CH:(m + 1) * CH]
                            for k in range(KC):
                                pe.matmul(dst, w_cols[:, k, mm * P:(mm + 1) * P], xn_t[:, k, :],
                                          start=(k == 0), stop=False)
                            ins = pe.matmul(dst, pick[:, mm * P:(mm + 1) * P], others_t[:, :],
                                            start=False, stop=True)
                        ins.then_inc(ring_filled, 1)
                    elif stage == "columns":
                        pe.wait_ge(ring_drained, ring_n + (rings + 2))
                        for t in range(CT):
                            for m in range(EM):
                                ins = pe.matmul(bank[:, t * C:(t + 1) * C], act_t[:, m, t * P:(t + 1) * P],
                                                w_proj[:, m, :], start=(m == 0), stop=(m == EM - 1))
                        ins.then_inc(bank_filled, 1)
                    elif stage == "o_turn":
                        pe.wait_ge(o_out, b * (2 * NG) + (2 * g + arg + 2))
                        for i in range(4):
                            ins = pe.transpose(bank[:, i * P:(i + 1) * P], o_sb[:, i * P:(i + 1) * P], ident[:, :])
                        ins.then_inc(bank_filled, 1)
                    elif stage == "y_turn":
                        for t in range(CT):
                            for k in range(KC):
                                ins = pe.transpose(bank[:, (t * KC + k) * P:(t * KC + k + 1) * P],
                                                   y[:, arg * CT + t, k * P:(k + 1) * P], ident[:, :])
                        ins.then_inc(bank_filled, 1)
                    elif stage == "project":
                        for t in range(CT):
                            for k in range(KC):
                                ins = pe.matmul(bank[:, t * C:(t + 1) * C], y_t[:, k, t * P:(t + 1) * P],
                                                w_out[:, k, :], start=(k == 0), stop=(k == KC - 1))
                        ins.then_inc(bank_filled, 1)

            run(pe, body)

        @block.vector
        def _(dve):
            dve.sem_inc(rows_drained, 2)
            dve.sem_inc(inv_ready, 1)
            dve.wait_ge(weights_in, LOADS * 16)
            emb = act_t[0:E, 0, :]
            dve.tensor_tensor_reduce(y2n[0:E, 0, :], emb, emb, 1.0, 0.0, ALU.mult, ALU.add,
                                     norm[0:E, 0, 0:1]).then_inc(embedded, 1)
            dve.wait_ge(embedded, 3)
            dve.tensor_scalar(y2n[0:E, 1, :], emb, norm[0:E, 2, 0:1], None, ALU.mult).then_inc(embedded, 1)
            dve.wait_ge(filled, FILLS)
            dve.wait_ge(bank_filled, 3)
            dve.wait_ge(near_in, 32)

            def body(stages, b, bank_n, ring_n):
                for stage, g, arg, banks, rings in stages:
                    fb, c, n = chunk_of(b, g)
                    ab, ag, gi = next_group(b, g)
                    if stage == "score":
                        s, h = arg
                        if s not in BIASED:
                            continue
                        dve.wait_ge(ring_filled, ring_n + (rings + 1))
                        near = near_cols[:, g * GH + h, :]
                        tile = ring[rings % 2]
                        if s in (0, 4):
                            two = tile[:, :].rearrange("p (a n) -> p a n", a=2)[:, :, 0:2 * P]
                            ins = dve.tensor_tensor(two, two, near.rearrange("p (a n) -> p a n", a=1)
                                                    .to_broadcast((P, 2, 2 * P)), ALU.add)
                        elif s in (1, 5):
                            dve.tensor_tensor(tile[:, 0:2 * P], tile[:, 0:2 * P], near, ALU.add)
                            ins = dve.tensor_tensor(tile[:, 2 * P:3 * P], tile[:, 2 * P:3 * P], near[:, 0:P], ALU.add)
                        else:
                            ins = dve.tensor_tensor(tile[:, HALF:HALF + P], tile[:, HALF:HALF + P],
                                                    near[:, P:2 * P], ALU.add)
                        ins.then_inc(ring_biased, 1)
                    elif stage == "row":
                        h, k = arg
                        qb, part = ROWS[k]
                        i = gi * (GH * len(ROWS)) + (h * len(ROWS) + k)
                        tile = row_ring[(h * len(ROWS) + k) % 2]
                        at = h * NT + qb
                        far = max(qb - 1, 0) * P
                        dve.wait_ge(rows_filled, i + 1)
                        if part == 0:
                            if far:
                                w = min(far, 2 * P)
                                dve.tensor_reduce(maxima[:, 1, at:at + 1], tile[:, 2 * P:2 * P + w], AX.X, ALU.max)
                            w = (qb + 1) * P - far
                            if not far:
                                alone(dve)
                            dve.tensor_tensor_reduce(tile[:, 0:w], tile[:, 0:w],
                                                     near_rows[:, ag * GH + h, 2 * P - w:2 * P], 1.0, LOWEST,
                                                     ALU.add, ALU.max, maxima[:, 0, at:at + 1]) \
                                .then_inc(rows_drained, 1)
                        else:
                            dve.tensor_reduce(maxima[:, 2, at:at + 1], tile[:, 0:far - 2 * P], AX.X, ALU.max) \
                                .then_inc(rows_drained, 1)
                    elif stage == "shift":
                        step = lambda k: dve.wait_ge(shift_step, gi * 6 + k)
                        dve.wait_ge(rows_drained, gi * (GH * len(ROWS)) + (GH * len(ROWS) + 2))
                        dve.tensor_reduce(shift[:, :], maxima[:, :, :].rearrange("p k j -> p j k"), AX.X, ALU.max,
                                          negate=True).then_inc(shift_step, 1)
                        step(1)
                        dve.tensor_copy(shift_p[:, 0, :], shift[:, :]).then_inc(shift_step, 1)
                        step(2)
                        dve.tensor_tensor(shift_l[:, 0, :], shift[:, :], shift_p[:, 0, :], ALU.subtract) \
                            .then_inc(shift_step, 1)
                        step(3)
                        dve.tensor_copy(shift_p[:, 1, :], shift_l[:, 0, :]).then_inc(shift_step, 1)
                        step(4)
                        dve.tensor_tensor(shift_l[:, 1, :], shift_l[:, 0, :], shift_p[:, 1, :], ALU.subtract) \
                            .then_inc(shift_step, 1)
                        step(5)
                        dve.tensor_copy(shift_p[:, 2, :], shift_l[:, 1, :]).then_inc(shift_step, 1)
                    elif stage == "o_turn":
                        k = b * (2 * NG) + (2 * g + arg)
                        o4 = bank[:, :].rearrange("p (i h e) -> p i h e", h=GH, e=32)
                        dve.wait_ge(bank_filled, bank_n + (banks + 1))
                        dve.reciprocal(inv[:, :, :], o4[:, :, :, D]).then_inc(inv_ready, 1)
                        dve.wait_ge(inv_ready, k + 2)
                        dst = y[:, arg * 4:(arg + 1) * 4, g * GH * D:(g + 1) * GH * D]
                        dve.tensor_tensor(dst.rearrange("p i (h d) -> p i h d", d=D), o4[:, :, :, 0:D],
                                          inv[:, :, :].rearrange("p i (h o) -> p i h o", o=1)
                                          .to_broadcast((P, 4, GH, D)), ALU.mult).then_inc(bank_drained, 1)
                    elif stage == "stats":
                        dve.wait_ge(x_in[c % 2], (fb * (NC // 2) + (c // 2 + 1)) * 16)
                        for t in range(CT):
                            ins = dve.bn_stats(stats[:, t, :], x[:, c % 2, t, :])
                        ins.then_inc(stats_done, 1)
                        dve.wait_ge(stats_done, n + 1)
                        alone(dve)
                        for t in range(CT):
                            ins = dve.bn_aggr(moments[:, t, :], stats[:, t, :])
                        ins.then_inc(moments_ready, 1)
                    elif stage == "center":
                        dve.wait_ge(rstd_ready, n + 1)
                        for t in range(CT):
                            ins = dve.tensor_scalar(xn[:, t, :], x[:, c % 2, t, :], moments[:, t, 0:1],
                                                    rstd[:, t:t + 1], ALU.subtract, ALU.mult)
                        ins.then_inc(xn_ready, 1)
                    elif stage == "qk":
                        dve.wait_ge(bank_filled, bank_n + (banks + 1))
                        wait(dve, rot_ready, n * CT + (arg + 1 - CT))
                        dve.tensor_tensor(qk[:, arg, :], bank[:, :], b_qkv[:, 0:2 * C], ALU.add) \
                            .then_inc(bank_drained, 1)
                    elif stage == "v":
                        dve.wait_ge(bank_filled, bank_n + (banks + 1))
                        wait(dve, v_out, n * 16)
                        dve.tensor_tensor(v[:, arg, :], bank[:, 0:C], b_qkv[:, 2 * C:3 * C], ALU.add) \
                            .then_inc(v_ready, 1)
                        dve.wait_ge(norm_step, n * NORM_STEPS + 5)
                        dve.tensor_scalar(like[:, arg, :], bank[:, C:C + E], norm[:, 4, arg:arg + 1], 0.5,
                                          ALU.mult, ALU.add).then_inc(bank_drained, 1)
                    elif stage == "gate":
                        dve.wait_ge(bank_filled, bank_n + (banks + 1))
                        dve.tensor_tensor(gate_in[:, :, :], bank[:, 0:CT * E].rearrange("p (t e) -> p t e", e=E),
                                          b_gate[:, :].rearrange("p (o e) -> p o e", o=1)
                                          .to_broadcast((P, CT, E)), ALU.add).then_inc(bank_drained, 1)
                    elif stage == "choose":
                        def each(col):
                            return col.rearrange("p (t o) -> p t o", o=1).to_broadcast((P, CT, E))
                        step = lambda k: dve.wait_ge(chosen, n * CHOSEN_STEPS + k)
                        dve.wait_ge(tanh_ready, n + 1)
                        dve.scalar_tensor_tensor(out=logits[:, :, :], in0=gate_th[:, :, :], scalar=0.5,
                                                 in1=like[:, :, :], op0=ALU.mult, op1=ALU.add).then_inc(chosen, 1)
                        step(1)
                        dve.tensor_reduce(top[:, :], logits[:, :, :], AX.X, ALU.max).then_inc(chosen, 1)
                        step(2)
                        dve.tensor_tensor(tied[:, :, :], logits[:, :, :], each(top[:, :]), ALU.is_equal) \
                            .then_inc(chosen, 1)
                        dve.tensor_tensor(below[:, :, :], logits[:, :, :], each(top[:, :]), ALU.subtract) \
                            .then_inc(chosen, 1)
                        step(3)
                        dve.tensor_tensor(ranked[:, :, :], tied[:, :, :],
                                          rank[:, :].rearrange("p (o e) -> p o e", o=1).to_broadcast((P, CT, E)),
                                          ALU.mult).then_inc(chosen, 1)
                        step(5)
                        dve.tensor_reduce(first[:, :], ranked[:, :, :], AX.X, ALU.max).then_inc(chosen, 1)
                        step(6)
                        dve.tensor_tensor(others[:, :, :], ranked[:, :, :], each(first[:, :]), ALU.not_equal) \
                            .then_inc(chosen, 1)
                    elif stage == "mask_turn":
                        dve.wait_ge(share_ready, n + 1)
                        dve.tensor_reduce(total[:, :], shares[:, :, :], AX.X, ALU.add).then_inc(chosen, 1)
                        dve.wait_ge(chosen, n * CHOSEN_STEPS + 8)
                        dve.reciprocal(weight[:, :], total[:, :]).then_inc(weight_ready, 1)
                    elif stage == "qk_turn":
                        dve.wait_ge(hi_ready, n * CT + (arg + 1))
                        wait(dve, lo_ready, n * CT + arg)
                        dve.tensor_tensor(left[:, :, :], bank[:, :].rearrange("p (q n) -> p q n", n=P),
                                          parts[0][:, :, arg * P:(arg + 1) * P], ALU.subtract) \
                            .then_inc(bank_drained, 1)
                    elif stage == "columns":
                        dve.wait_ge(bank_filled, bank_n + (banks + 1))
                        dve.wait_ge(weight_ready, n + 1)
                        dve.wait_ge(skip_ready, n + 1)
                        for t in range(CT):
                            ins = dve.scalar_tensor_tensor(out=y2[:, t, :], in0=bank[:, t * C:(t + 1) * C],
                                                           scalar=weight[:, t:t + 1], in1=skip[:, t, :],
                                                           op0=ALU.mult, op1=ALU.add)
                        ins.then_inc(bank_drained, 1)
                        dve.wait_ge(bank_drained, bank_n + (banks + 2))
                        for t in range(CT):
                            ins = dve.bn_stats(stats2[:, t, :], y2[:, t, :])
                        ins.then_inc(stats2_done, 1)
                        dve.wait_ge(stats2_done, n + 1)
                        alone(dve)
                        for t in range(CT):
                            ins = dve.bn_aggr(moments2[:, t, :], stats2[:, t, :])
                        ins.then_inc(moments2_ready, 1)
                    elif stage == "finish":
                        dve.wait_ge(rstd2_ready, n)
                        wait(dve, rest_all, n - 1)
                        for t in range(CT):
                            ins = dve.tensor_scalar(y2n[:, t, :], y2[:, t, :], moments2[:, t, 0:1],
                                                    rstd2[:, t:t + 1], ALU.subtract, ALU.mult)
                        ins.then_inc(y2n_ready, 1)
                    elif stage == "project":
                        dve.wait_ge(bank_filled, bank_n + (banks + 1))
                        dve.wait_ge(rest_in_done[arg % 2], b * (NC // 2 * 16) + (arg // 2 + 1) * 16)
                        sum_ = result[:, arg % 2].rearrange("p t n -> p (t n)")
                        dve.tensor_tensor(sum_, bank[:, :], sum_, ALU.add) \
                            .then_inc(bank_drained, 1)

            run(dve, body)


LOADS = 23
FILLS = 9


_INS = {
    "x": "L0_attn_x", "Wq": "L0_attn_Wq", "bq": "L0_attn_bq", "Wk": "L0_attn_Wk", "bk": "L0_attn_bk",
    "Wv": "L0_attn_Wv", "bv": "L0_attn_bv", "Wp": "L0_attn_Wp", "bp": "L0_attn_bp",
    "rel_bias_table": "L0_attn_rel_bias_table", "col_emb": "L0_ffn_col_emb", "gate_w1": "L0_ffn_gate_w1",
    "gate_b1": "L0_ffn_gate_b1", "gate_w2": "L0_ffn_gate_w2", "gate_b2": "L0_ffn_gate_b2",
    "W_cols": "L0_ffn_W_cols", "b_cols": "L0_ffn_b_cols", "proj_w": "L0_ffn_proj_w",
    "proj_b": "L0_ffn_proj_b", "ln_g": "L0_ffn_ln_g", "ln_b": "L0_ffn_ln_b",
}


def shape_constants():
    f = np.float32
    freq = f(1.0) / f(10000.0) ** (np.arange(0, D, 2, dtype=f) / f(D))
    angle = np.arange(T, dtype=f)[:, None] * freq.astype(f)[None, :]
    cos, sin = np.cos(angle).astype(f), np.sin(angle).astype(f)
    rotary = np.stack([cos, sin, -sin], axis=1).reshape(NT, P, 3, D // 2).transpose(1, 0, 2, 3)
    n = np.arange(N_OFF) - P
    exact = BUCKETS // 2
    large = exact + (np.log(np.maximum(n, 1).astype(f) / f(exact)) / f(np.log(128 / exact)) * f(BUCKETS - exact)) \
        .astype(np.int32)
    bucket = np.where(n < exact, np.maximum(n, 0), np.minimum(large, BUCKETS - 1))
    picks = np.zeros((BUCKETS + 1, N_OFF), f)
    ok = n >= 0
    picks[bucket[ok], np.nonzero(ok)[0]] += 1
    picks[BUCKETS - 1, ok] -= 1
    picks[BUCKETS, ~ok] = 1
    assert not picks[:, n >= P + 1].any()
    neuron = np.arange(E * N) // N
    return {
        "ident": np.eye(P, dtype=f),
        "rank": (E - np.arange(E)).astype(f),
        "rotary": np.ascontiguousarray(rotary),
        "offset_picks": np.ascontiguousarray(np.stack([picks, picks[:, ::-1]], axis=1)),
        "pick": np.where(np.arange(E)[:, None] == neuron[None, :], f(OFF), f(0)).astype(f),
    }


def kernel(**inputs):
    import concourse.bacc as _bacc
    from concourse.bass_utils import run_bass_kernel_spmd as _run

    nc = _bacc.Bacc("TRN2", target_bir_lowering=False, num_devices=1)
    arrays, args = {}, {}
    given = {k: np.ascontiguousarray(inputs[name]) for k, name in _INS.items()}
    for name, arr in list(given.items()) + list(shape_constants().items()):
        arrays[f"in_{name}_dram"] = arr
        args[name] = nc.dram_tensor(f"in_{name}_dram", arr.shape, mybir.dt.from_np(arr.dtype),
                                    kind="ExternalInput").ap()
    out = nc.dram_tensor("out_0_dram", (B, T, C), F32, kind="ExternalOutput").ap()
    layer_kernel(nc, args, out)
    r = _run(nc, [arrays], core_ids=[0])
    return r.results[0]["out_0_dram"]
```

```python
from contextlib import ExitStack

import numpy as np

import concourse.bass as bass
from concourse import mybir
from concourse.alu_op_type import AluOpType as ALU

F32 = mybir.dt.float32
BF16 = mybir.dt.bfloat16
ACT = mybir.ActivationFunctionType
AX = mybir.AxisListType

P = 128
B, T, C = 8, 1024, 256
H, D = 16, 16
GH = 4
NG = H // GH
NT = T // P
CT = 2
CH = CT * P
NC = T // CH
KC = C // P
E = 16
N = 64
EM = E * N // P
BUCKETS = 32
LOWEST = -3.0e38
OFF = -1.0e30
STACK = 6 * D
Q_PARTS = (0, 0, 0, 1, 1, 2)
K_PARTS = (0, 1, 2, 0, 1, 0)
RUNS = ((0, 3), (3, 2), (5, 1))
LEAD = NG + 1
HALF = 512
EXTRA = E
QKV = 3 * C + EXTRA

STEPS = [
    (0, [(0, 0, 0)], 512), (0, [(1, 128, 0)], 384), (0, [(2, 256, 0), (3, 384, 256)], 384),
    (1, [(0, 512, 0)], 512), (1, [(1, 512, 0)], 512), (1, [(2, 512, 0)], 512), (1, [(3, 512, 0)], 512),
    (1, [(4, 512, 0)], 512), (1, [(5, 640, 0)], 384), (1, [(6, 768, 0), (7, 896, 256)], 384),
]
NS = len(STEPS)
SLOTS = NS * GH
BIASED = [0, 1, 2, 6, 7, 8, 9]
LAST_STEP = (2, NS - 1)
RING = 3
PROBS = 4
SETUP = 2

ROWS = [(qb, part) for qb in range(NT) for part in range(1 if qb < 4 else 2)]
ALL_ROWS = [(h, k) for h in range(GH) for k in range(len(ROWS))]
PV_AFTER = 8
SPREAD = 4
SHEAR = 3 * P
N_OFF = 512
CHOSEN_STEPS = 8
NORM_STEPS = 5
M_PIECE = 2
C_PIECES = CT * EM // M_PIECE
N_PIECES = 2

BESIDE = {1: [('columns', 3)],
          2: [('widen', None), ('columns', 4)],
          3: [('center', None)],
          4: [('columns', 5)],
          5: [('columns', 6)],
          6: [('columns', 7)],
          7: [('x_turn', None)],
          9: [('y2_stats', None)],
          10: [('skip', None)],
          11: [('qk_begun', 0), ('qk', 0)],
          12: [('v', 0)],
          15: [('finish', None), ('qk_begun', 1)],
          16: [('qk', 1)],
          17: [('hidden', None)],
          19: [('v', 1)],
          21: [('gate', None), ('o_turn', 0)],
          23: [('qk_turn', 0), ('choose', None)],
          25: [('left', 0), ('tie', None), ('middle', 0)],
          26: [('choice', None), ('y_turn', 0)],
          28: [('project_begun', 0)],
          29: [('project', 0)],
          30: [('qk_turn', 1)],
          31: [('left', 1), ('mask_turn', None)],
          32: [('y_turn', 1)],
          34: [('middle', 1)],
          35: [('project_begun', 1)],
          37: [('project', 1)]}
OPENING = [("stats", None), ("columns", 0), ("columns", 1), ("columns", 2)]
ALONE = ([("stats", None), ("center", None), ("x_turn", None)] + [("columns", k) for k in range(C_PIECES)]
         + [("qk_begun", 0), ("qk", 0), ("qk_begun", 1), ("qk", 1), ("y2_stats", None), ("skip", None),
            ("hidden", None), ("v", 0), ("gate", None), ("v", 1), ("choose", None), ("qk_turn", 0),
            ("left", 0), ("tie", None), ("choice", None), ("finish", None), ("middle", 0), ("qk_turn", 1),
            ("left", 1), ("mask_turn", None)]
         + [("neurons", (k, m)) for k in range(2) for m in range(N_PIECES)] + [("middle", 1)]
         + [("neurons", (k, m)) for k in range(2, 4) for m in range(N_PIECES)])
CLOSING = [("load", None), ("neurons", (0, 0)), ("neurons", (0, 1)), ("pv", NS - 1), ("o_out", 1),
           ("neurons", (1, 0)), ("neurons", (1, 1)), ("neurons", (2, 0)), ("shift", None),
           ("neurons", (2, 1)), ("neurons", (3, 0)), ("neurons", (3, 1)), ("o_turn", 1), ("shift_turn", None)]
FRONT = {"stats", "center", "x_turn", "qk_begun", "qk", "v", "hidden", "gate", "choose", "tie", "choice",
         "qk_turn", "mask_turn", "left", "middle", "neurons", "skip"}
FRONT_LATER = {"columns", "y2_stats", "finish"}
BANKED = {"x_turn", "qk", "v", "gate", "qk_turn", "mask_turn", "o_turn", "shift_turn",
          "columns", "y_turn", "project"}
PE_TIME = {"score": 2, "pv": 9, "columns": 9, "neurons": 10, "x_turn": 4, "qk": 9, "v": 9, "qk_begun": 9,
           "project_begun": 9, "hidden": 9, "qk_turn": 4, "mask_turn": 2, "o_turn": 4, "y_turn": 4,
           "project": 9}
DVE_TIME = {"score": 2, "center": 7, "qk": 6, "v": 5, "gate": 1, "choose": 3, "tie": 4, "choice": 3,
            "y2_stats": 10, "mask_turn": 3, "left": 6, "o_turn": 6, "project": 6, "finish": 7, "stats": 10}


def with_rows(plan, first, last, rows):
    spare, most = [], 0
    for at, (stage, arg) in enumerate(plan):
        if first <= at < last:
            dve = 8 if (stage, arg) == ("columns", C_PIECES - 1) else DVE_TIME.get(stage, 0)
            most += PE_TIME.get(stage, 0) - dve + (SPREAD if stage == "score" else 0)
        spare.append(most)
    whole, placed, out = max(spare[first:last]), 0, []
    for at, p in enumerate(plan):
        if at == first:
            out += [("row", row) for row in rows[:2]]
            placed = 2
        if at == last:
            out += [("row", row) for row in rows[placed:]]
            placed = len(rows)
        out.append(p)
        while first <= at < last and placed < len(rows) * spare[at] // whole:
            out.append(("row", rows[placed]))
            placed += 1
    return out


NEEDS = {"qk_begun": "x_turn", "qk": "x_turn", "v": "x_turn", "hidden": "x_turn",
         "project_begun": "y_turn", "project": "y_turn", "neurons": "mask_turn",
         "y_turn": "o_turn", "y2_stats": "columns", "choose": "v"}


class Order:

    def __init__(self):
        self.stages, self.banks, self.rings, self.used = [], 0, 0, {}

    def add(self, stage, g, arg=None):
        needs = self.used.get(NEEDS.get(stage))
        if stage in ("left", "middle"):
            needs = self.used["qk_turn", arg]
        if stage == "gate":
            needs = self.used["hidden"]
        if stage == "pv":
            needs = self.used["score", arg]
        self.stages.append((stage, g, arg, self.banks, self.rings, needs))
        ringed = stage in ("score", "neurons", "hidden")
        self.used[stage] = self.rings if ringed else self.banks
        self.used[stage, arg[0] if stage == "score" else arg] = self.used[stage]
        self.banks += stage in BANKED and not (stage == "columns" and arg < C_PIECES - 1)
        self.rings += ringed and not (stage == "neurons" and arg[1] < N_PIECES - 1)


def iteration(batch):
    o = Order()
    for g in range(NG):
        has_front = batch + (g + LEAD) // NC < B
        has_later = batch + (g + LEAD - 1) // NC < B
        has_next = not (batch == B - 1 and g == NG - 1)
        has_load = batch < B - 1 or g + 2 < NG

        plan = list(OPENING)
        for i in range(SLOTS):
            s, h = divmod(i, GH)
            plan.append(("score", (s, h)))
            if i >= PV_AFTER and (i - PV_AFTER) % GH == 0:
                done = (i - PV_AFTER) // GH
                plan.append(("pv", done))
                if done == LAST_STEP[0]:
                    plan.append(("o_out", 0))
            plan += [(stage, arg + 2 * (g == 0) if stage in ("y_turn", "project_begun", "project") else arg)
                     for stage, arg in BESIDE.get(i, [])]
        plan += [("pv", s) for s in range((SLOTS - 1 - PV_AFTER) // GH + 1, NS - 1)]
        plan += CLOSING

        def here(stage):
            return (has_front if stage in FRONT else has_later if stage in FRONT_LATER
                    else has_next if stage in ("widen", "shift", "shift_turn")
                    else has_load if stage == "load"
                    else (g == NG - 1 or (g == 0 and batch > 0)) if stage in ("y_turn", "project_begun", "project")
                    else True)
        plan = [(stage, arg) for stage, arg in plan if here(stage)]
        if has_next:
            plan = with_rows(plan, 0, plan.index(("shift", None)), ALL_ROWS)
        for stage, arg in plan:
            o.add(stage, g, arg)
    if batch == B - 1:
        for k in range(NC // 2, NC):
            o.add("y_turn", NG - 1, k)
            o.add("project_begun", NG - 1, k)
            o.add("project", NG - 1, k)
    return o


def prologue():
    o = Order()
    for g in range(-LEAD, 0):
        plan = [p for p in ALONE if p[0] in FRONT or g > -LEAD]
        if g == -1:
            o.add("load", -2)
            plan = with_rows(plan, len(plan) // 5, len(plan) - 1, ALL_ROWS)
        for stage, arg in plan:
            o.add(stage, g, arg)
    o.add("widen", -1)
    o.add("load", -1)
    o.add("shift", -1)
    o.add("shift_turn", -1)
    return o


def layer_kernel(nc, a, out):
    ctx = ExitStack()
    with ctx:
        def sb(name, shape, dt=F32):
            return ctx.enter_context(nc.sbuf_tensor(name, shape, dt))

        def pb(name, shape, dt=F32):
            return ctx.enter_context(nc.psum_tensor(name, shape, dt))

        def sem(name):
            return ctx.enter_context(nc.semaphore(name))

        parts_d = nc.dram_tensor("parts_d", (B, 3, 2 * KC, P, T), BF16, kind="Internal").ap()
        v_d = nc.dram_tensor("v_d", (B, P, NT, C), F32, kind="Internal").ap()
        rest_d = nc.dram_tensor("rest_d", (B, P, NT, C), F32, kind="Internal").ap()
        offsets_d = nc.dram_tensor("offsets_d", (2, H, N_OFF), F32, kind="Internal").ap()
        sheared_d = nc.dram_tensor("sheared_d", (2, H, P, SHEAR), F32, kind="Internal").ap()

        ident = sb("ident", [P, P])
        ident_b = sb("ident_b", [P, P], BF16)
        w_qkv = sb("w_qkv", [P, KC, QKV])
        w_out = sb("w_out", [P, KC, C])
        w_hid = sb("w_hid", [P, KC, P])
        w_gate = sb("w_gate", [P, E])
        w_cols = sb("w_cols", [P, KC, E * N])
        w_proj = sb("w_proj", [P, EM, C])
        b_qkv = sb("b_qkv", [P, 3 * C])
        b_gate = sb("b_gate", [P, E])
        b_hid = sb("b_hid", [P, 1])
        b_cols = sb("b_cols", [P, EM])
        b_proj = sb("b_proj", [P, C])
        gain = sb("gain", [P, C])
        b_rest = sb("b_rest", [P, C])
        rank = sb("rank", [P, E])
        power = sb("power", [P, CT])
        rotary = sb("rotary", [P, NT, 3, D // 2])
        pick = sb("pick", [E, EM * P], BF16)
        near_rows = sb("near_rows", [P, H, 2 * P])
        near_cols = sb("near_cols", [P, H, 2 * P])

        x = sb("x", [P, 2, CT, C])
        stats = sb("stats", [P, CT, 6])
        moments = sb("moments", [P, CT, 2])
        rstd = sb("rstd", [P, CT])
        norm = sb("norm", [P, 6, CT])
        xn = sb("xn", [P, CT, C])
        xn_t = sb("xn_t", [P, KC, CH])
        skip = sb("skip", [P, CT, C])
        rest = sb("rest", [P, CT, C])
        qk = sb("qk", [P, CT, 2 * C])
        swapped = sb("swapped", [P, 2 * C])
        rot = sb("rot", [P, CT, 2 * C])
        parts = [sb(f"part{i}", [P, 2 * KC, CH], BF16) for i in range(3)]
        left = sb("left", [P, 2 * KC, P])
        v = sb("v", [P, CT, C])
        like = sb("like", [P, CT, E])
        hid_t = sb("hid_t", [P, CH])
        gate_in = sb("gate_in", [P, CT, E])
        gate_th = sb("gate_th", [P, CT, E])
        logits = sb("logits", [P, CT, E])
        top = sb("top", [P, CT])
        tied = sb("tied", [P, CT, E])
        ranked = sb("ranked", [P, CT, E])
        first = sb("first", [P, CT])
        others = sb("others", [P, CT, E])
        below = sb("below", [P, CT, E])
        shares = sb("shares", [P, CT, E])
        total = sb("total", [P, CT])
        weight = sb("weight", [P, CT])
        others_t = sb("others_t", [E, CH], BF16)
        act_t = sb("act_t", [P, EM, CH])
        y2 = sb("y2", [P, CT, C])
        stats2 = sb("stats2", [P, CT, 6])
        moments2 = sb("moments2", [P, CT, 2])
        rstd2 = sb("rstd2", [P, CT])
        y2n = sb("y2n", [P, CT, C])

        stack_q = [sb(f"stack_q{i}", [STACK + 3, GH, T], BF16) for i in range(2)]
        stack_k = [sb(f"stack_k{i}", [STACK + 3, GH, T], BF16) for i in range(2)]
        v_in = sb("v_in", [P, NT, GH * D])
        v_aug = [sb(f"v_aug{i}", [P, NT, GH, 32]) for i in range(2)]
        maxima = sb("maxima", [P, 3, GH * NT])
        shift = sb("shift", [P, GH * NT])
        shift_l = sb("shift_l", [P, 2, GH * NT])
        shift_p = sb("shift_p", [P, 3, GH * NT], BF16)
        shift_t = sb("shift_t", [3 * GH * NT, P], BF16)
        probs = sb("probs", [P, PROBS, GH, HALF])
        o_sb = sb("o_sb", [P, HALF])
        inv = sb("inv", [P, 4, GH])
        y = sb("y", [P, NT, C])
        y_t = sb("y_t", [P, KC, CH])
        result = sb("result", [P, 2, CT, C])

        ring = [pb(f"scores{i}", [P, HALF]) for i in range(RING)]
        row_ring = [pb(f"rows{i}", [P, 512]) for i in range(2)]
        o_bank = pb("o_bank", [P, HALF])
        bank_pair = [pb(f"bank{i}", [P, 512]) for i in range(2)]

        weights_in = sem("weights_in")
        columns_in = sem("columns_in")
        filled = sem("filled")
        embedded = sem("embedded")
        rest_bias = sem("rest_bias")
        cast = sem("cast")
        offsets_made = sem("offsets_made")
        offsets_out = sem("offsets_out")
        sheared = sem("sheared")
        near_in = sem("near_in")
        x_in = [sem(f"x_in{i}") for i in range(2)]
        bank_filled = [sem(f"bank_filled{i}") for i in range(2)]
        bank_drained = [sem(f"bank_drained{i}") for i in range(2)]
        ring_filled = sem("ring_filled")
        ring_biased = sem("ring_biased")
        ring_drained = sem("ring_drained")
        rows_filled = sem("rows_filled")
        rows_drained = sem("rows_drained")
        stats_done = sem("stats_done")
        moments_ready = sem("moments_ready")
        rstd_ready = sem("rstd_ready")
        norm_step = sem("norm_step")
        norm2_step = sem("norm2_step")
        xn_ready = sem("xn_ready")
        skip_ready = sem("skip_ready")
        rest_ready = sem("rest_ready")
        rope_step = sem("rope_step")
        rot_ready = sem("rot_ready")
        v_ready = sem("v_ready")
        hi_ready = sem("hi_ready")
        mid_ready = sem("mid_ready")
        lo_ready = sem("lo_ready")
        parts_out = [sem(f"parts_out{i}") for i in range(3)]
        v_out = sem("v_out")
        rest_out = sem("rest_out")
        tanh_ready = sem("tanh_ready")
        chosen = sem("chosen")
        share_ready = sem("share_ready")
        weight_ready = sem("weight_ready")
        stats2_done = sem("stats2_done")
        moments2_ready = sem("moments2_ready")
        rstd2_ready = sem("rstd2_ready")
        y2n_ready = sem("y2n_ready")
        scaled = sem("scaled")
        rest_all = sem("rest_all")
        stack_in = [sem(f"stack_in{i}") for i in range(2)]
        v_in_done = sem("v_in_done")
        v_aug_ready = sem("v_aug_ready")
        shift_step = sem("shift_step")
        counted = sem("counted")
        shift_in = sem("shift_in")
        probs_used = sem("probs_used")
        o_out = sem("o_out")
        inv_ready = sem("inv_ready")
        rest_in_done = [sem(f"rest_in{i}") for i in range(2)]
        result_out = [sem(f"result_out{i}") for i in range(2)]

        parts_of_run = [prologue(), iteration(0), iteration(1), iteration(B - 2), iteration(B - 1)]
        LOOPS = B - 3
        assert parts_of_run[2].banks % 2 == 0 and parts_of_run[2].rings % RING == 0

        def run(engine, body):
            banks, rings = 0, 0
            for order, b in zip(parts_of_run, (-1, 0, None, B - 2, B - 1)):
                if b is None:
                    with engine.Fori(1, 1 + LOOPS) as b:
                        half = order.banks // 2
                        body(order.stages, b, (b * half + (banks // 2 - half + SETUP), banks % 2),
                             (b * order.rings + (rings - order.rings), rings % RING))
                    banks += LOOPS * order.banks
                    rings += LOOPS * order.rings
                else:
                    body(order.stages, b, (banks // 2 + SETUP, banks % 2), (rings, rings % RING))
                    banks += order.banks
                    rings += order.rings

        def bank_use(bank_n, use):
            return (use + bank_n[1]) % 2, bank_n[0] + (use + bank_n[1]) // 2

        def projected(b, g):
            return b if g == NG - 1 else b - 1

        def chunk_of(b, g):
            n = g + LEAD
            if g < 0:
                return n // NC, n % NC, n
            fb, c = b + n // NC, n % NC
            return fb, c, fb * NC + c

        def next_group(b, g):
            ab, ag = (0, 0) if g < 0 else (b, g + 1) if g + 1 < NG else (b + 1, 0)
            return ab, ag, ab * NG + ag

        def loaded_group(b, g):
            tb, tg = (0, g + 2) if g < 0 else (b, g + 2) if g + 2 < NG else (b + 1, g + 2 - NG)
            return tb, tg, tb * NG + tg

        def wait(eng, s, value):
            if not isinstance(value, int) or value > 0:
                eng.wait_ge(s, value)

        def alone(eng):
            eng.sem_inc(counted, 1)

        block = ctx.enter_context(nc.Block())

        @block.sync
        def _(sp):
            def every(ap1d, n):
                return bass.AP(ap1d.tensor, 0, [[0, P], [1, n]])

            x_v = a["x"].rearrange("b (c t p) f -> b c p t f", c=NC, p=P)
            out_v = out.rearrange("b (c t p) f -> b c p t f", c=NC, p=P)

            def load_x(fb, c):
                wait(sp, xn_ready, fb * NC + c - 1)
                wait(sp, rest_ready, fb * NC + c - 1)
                alone(sp)
                sp.dma_start(x[:, c % 2], x_v[fb, c]).then_inc(x_in[c % 2], 16)

            first_in = [
                (ident[:, :], a["ident"]), (rank[:, :], every(a["rank"], E)),
                (rotary[:, :, :, :], a["rotary"]),
                (w_qkv[:, :, 0:C], a["Wq"].rearrange("(k p) n -> p k n", p=P)),
                (w_qkv[:, :, C:2 * C], a["Wk"].rearrange("(k p) n -> p k n", p=P)),
                (w_qkv[:, :, 2 * C:3 * C], a["Wv"].rearrange("(k p) n -> p k n", p=P)),
                (b_qkv[:, 0:C], every(a["bq"], C)), (b_qkv[:, C:2 * C], every(a["bk"], C)),
                (b_qkv[:, 2 * C:3 * C], every(a["bv"], C)),
                (w_hid[:, :, :], a["gate_w1"].rearrange("(k p) n -> p k n", p=P)),
                (b_hid[:, :], a["gate_b1"].rearrange("(p o) -> p o", o=1)),
                (w_gate[:, :], a["gate_w2"]), (b_gate[:, :], every(a["gate_b2"], E)),
                (b_proj[:, :], every(a["proj_b"], C)), (gain[:, :], every(a["ln_g"], C)),
                (b_rest[:, :], every(a["bp"], C)), (skip[:, 0, :], every(a["ln_b"], C)),
                (act_t[0:E, 0, :], a["col_emb"]),
                (act_t[0:E, 1:5, :].rearrange("p m n -> p (m n)"), a["pick"]),
                (y2[0:BUCKETS, 0, 0:H], a["rel_bias_table"]),
                (qk[0:BUCKETS + 1, :, :], a["offset_picks"])]
            assert len(first_in) == LOADS
            with nc.allow_non_contiguous_dma(reason="one bias per partition, once"):
                for dst, src in first_in:
                    sp.dma_start(dst, src).then_inc(weights_in, 16)
                load_x(0, 0)
                load_x(0, 1)
                sp.dma_start(w_out[:, :, :], a["Wp"].rearrange("(k p) n -> p k n", p=P)).then_inc(columns_in, 16)
                sp.dma_start(w_proj[:, :, :], a["proj_w"].rearrange("(m p) n -> p m n", p=P)) \
                    .then_inc(columns_in, 16)
                for k in range(KC):
                    sp.dma_start(w_cols[:, k, :].rearrange("p (c n) -> p c n", n=N),
                                 a["W_cols"][:, k * P:(k + 1) * P, :].rearrange("c p n -> p c n")) \
                        .then_inc(columns_in, 16)
                sp.dma_start(b_cols[:, :], bass.AP(a["b_cols"].tensor, 0, [[1, P], [P, EM]])) \
                    .then_inc(columns_in, 16)
            def store_rest(fb, c, n):
                mb, mc = (fb, c - 1) if c else (fb - 1, NC - 1)
                sp.wait_ge(rest_all, n)
                alone(sp)
                sp.dma_start(rest_d[mb, :, mc * CT:(mc + 1) * CT, :], rest[:, :, :]).then_inc(rest_out, 16)

            sp.sem_inc(result_out[0], 16)
            sp.sem_inc(result_out[1], 16)
            sp.wait_ge(offsets_made, 2)
            sp.dma_start(offsets_d.rearrange("r h n -> h r n"), rot[0:H, :, :]).then_inc(offsets_out, 16)
            sp.wait_ge(offsets_out, 16)
            for r in range(2):
                sp.dma_start(sheared_d[r], bass.AP(offsets_d.tensor, r * (H * N_OFF + P),
                                                   [[N_OFF, H], [0, P], [1, SHEAR]])).then_inc(sheared, 16)

            def load_near():
                sp.wait_ge(sheared, 32)
                for r, near in enumerate((near_cols, near_rows)):
                    sp.dma_start(near[:, :, :], bass.AP(sheared_d.tensor, r * H * P * SHEAR + P - r,
                                                        [[SHEAR - 1, P], [P * SHEAR, H], [1, 2 * P]])) \
                        .then_inc(near_in, 16)

            def body(stages, b, bank_n, ring_n):
                for stage, g, arg, banks, rings, needs in stages:
                    fb, c, n = chunk_of(b, g)
                    i, use = bank_use(bank_n, banks)
                    bank = bank_pair[i]
                    tile_n = ring_n[0] + rings
                    scores = ring[(rings + ring_n[1]) % RING]
                    ab, ag, gi = next_group(b, g)
                    if stage == "load":
                        tb, tg, ti = loaded_group(b, g)
                        for i in range(3):
                            sp.wait_ge(parts_out[i], (tb + 1) * (NC * 16))
                        sp.wait_ge(v_out, (tb + 1) * (NC * 16))
                        alone(sp)
                        if g >= 0:
                            sp.wait_ge(ring_filled, tile_n)
                        alone(sp)
                        half = slice((tg % 2) * GH * D, (tg % 2 + 1) * GH * D)
                        for first_r, n_r in RUNS:
                            rows_ = slice(first_r * D, (first_r + n_r) * D)
                            src = parts_d[tb, Q_PARTS[first_r]:Q_PARTS[first_r] + 1, tg // 2, half, :] \
                                .rearrange("r (d h) t -> r d (h t)", d=D).to_broadcast((n_r, D, GH * T))
                            sp.dma_start(stack_q[tg % 2][rows_].rearrange("p h t -> p (h t)"), src) \
                                .then_inc(stack_in[tg % 2], 16)
                            src = parts_d[tb, 0:n_r, KC + tg // 2, half, :] \
                                .rearrange("r (d h) t -> r d (h t)", d=D)
                            sp.dma_start(stack_k[tg % 2][rows_].rearrange("p h t -> p (h t)"), src) \
                                .then_inc(stack_in[tg % 2], 16)
                        wait(sp, v_aug_ready, ti)
                        alone(sp)
                        sp.dma_start(v_in[:, :, :], v_d[tb, :, :, tg * GH * D:(tg + 1) * GH * D]) \
                            .then_inc(v_in_done, 16)
                    elif stage == "v" and arg == 1:
                        sp.wait_ge(v_ready, n * CT + CT)
                        alone(sp)
                        sp.dma_start(v_d[fb, :, c * CT:(c + 1) * CT, :], v[:, :, :]).then_inc(v_out, 16)
                        if g > -LEAD:
                            store_rest(fb, c, n)
                        else:
                            load_near()
                    elif stage == "mask_turn":
                        if not isinstance(n, int) or n + 2 < B * NC:
                            load_x(*((fb, c + 2) if c + 2 < NC else (fb + 1, c + 2 - NC)))
                    elif stage == "middle" and arg == 1:
                        for i, ready in enumerate((hi_ready, mid_ready, lo_ready)):
                            sp.wait_ge(ready, n * CT + CT)
                            alone(sp)
                            sp.dma_start(parts_d[fb, i, :, :, c * CH:(c + 1) * CH].rearrange("q p t -> p q t"),
                                         parts[i][:, :, :]).then_inc(parts_out[i], 16)
                    elif stage == "finish" and isinstance(n, int) and n == B * NC:
                        store_rest(fb, c, n)
                    elif stage == "shift_turn":
                        sp.wait_ge(bank_drained[i], use + 2)
                        sp.dma_start(stack_q[ag % 2][STACK:STACK + 3].rearrange("r h (q t) -> r (h q) t", t=P),
                                     shift_t[:, :]).then_inc(shift_in, 16)
                    elif stage == "y_turn" and arg == 0:
                        sp.wait_ge(rest_out, (b + 1) * (NC * 16))
                        for k in range(2):
                            sp.wait_ge(result_out[k], b * (NC // 2 * 16) + 16)
                            alone(sp)
                            sp.dma_start(result[:, k], rest_d[b, :, k * CT:(k + 1) * CT, :]) \
                                .then_inc(rest_in_done[k], 16)
                    elif stage == "project":
                        pb = projected(b, g)
                        sp.wait_ge(bank_drained[i], use + 2)
                        alone(sp)
                        sp.dma_start(out_v[pb, arg], result[:, arg % 2]).then_inc(result_out[arg % 2], 16)
                        k = arg + 1
                        if 2 <= k < NC:
                            sp.wait_ge(result_out[k % 2], pb * (NC // 2 * 16) + (k // 2 + 1) * 16)
                            alone(sp)
                            sp.dma_start(result[:, k % 2], rest_d[pb, :, k * CT:(k + 1) * CT, :]) \
                                .then_inc(rest_in_done[k % 2], 16)

            run(sp, body)
            for i in range(2):
                sp.wait_ge(result_out[i], 16 + B * NC // 2 * 16)
                sp.wait_ge(parts_out[i], B * NC * 16)
            sp.wait_ge(parts_out[2], B * NC * 16)
            sp.wait_ge(v_out, B * NC * 16)
            sp.wait_ge(rest_out, B * NC * 16)

        @block.gpsimd
        def _(pool):
            fills = [(power[:, :], -0.5), (maxima[:, :, :], LOWEST),
                     (y2[BUCKETS:BUCKETS + 1, 0, 0:H], LOWEST)]
            for i in range(2):
                fills += [(v_aug[i][:, :, :, :], 0.0), (v_aug[i][:, :, :, D:D + 1], 1.0),
                          (stack_k[i][STACK:STACK + 3], 1.0)]
            assert len(fills) == FILLS
            for k, (dst, value) in enumerate(fills):
                wait(pool, filled, k)
                pool.memset(dst, value).then_inc(filled, 1)
            pool.wait_ge(embedded, 1)
            pool.tensor_scalar(norm[0:E, 1, 0:1], norm[0:E, 0, 0:1], 1e-24, None, ALU.max).then_inc(embedded, 1)
            pool.wait_ge(embedded, 2)
            pool.tensor_tensor(norm[0:E, 2, 0:1], norm[0:E, 1, 0:1], power[0:E, 0:1], ALU.pow) \
                .then_inc(embedded, 1)
            pool.wait_ge(weights_in, LOADS * 16)
            pool.tensor_tensor(b_rest[:, :], b_rest[:, :], skip[:, 0, :], ALU.add).then_inc(rest_bias, 1)
            pool.wait_ge(rest_bias, 1)
            pool.wait_ge(embedded, 4)

            def body(stages, b, bank_n, ring_n):
                for stage, g, arg, banks, rings, needs in stages:
                    fb, c, n = chunk_of(b, g)
                    i, use = bank_use(bank_n, banks)
                    bank = bank_pair[i]
                    tile_n = ring_n[0] + rings
                    scores = ring[(rings + ring_n[1]) % RING]
                    ab, ag, gi = next_group(b, g)
                    if stage == "stats":
                        wait(pool, rstd_ready, n)
                        pool.wait_ge(moments_ready, n + 1)
                        alone(pool)
                        pool.tensor_scalar(norm[:, 0, :], moments[:, :, 1], 1e-5, None, ALU.add) \
                            .then_inc(norm_step, 1)
                        pool.wait_ge(norm_step, n * NORM_STEPS + 1)
                        pool.tensor_tensor(rstd[:, :], norm[:, 0, :], power[:, :], ALU.pow) \
                            .then_inc(rstd_ready, 1)
                    elif stage == "finish":
                        pool.wait_ge(y2n_ready, n)
                        for t in range(CT):
                            ins = pool.tensor_tensor(y2n[:, t, :], y2n[:, t, :], gain[:, :], ALU.mult)
                        ins.then_inc(scaled, 1)
                        pool.wait_ge(scaled, n)
                        pool.tensor_tensor(rest[:, :, :], rest[:, :, :], y2n[:, :, :], ALU.add) \
                            .then_inc(rest_all, 1)
                    elif stage == "x_turn":
                        pool.wait_ge(rstd_ready, n + 1)
                        pool.wait_ge(norm_step, n * NORM_STEPS + 1)
                        pool.tensor_tensor(norm[:, 1, :], rstd[:, :], rstd[:, :], ALU.mult).then_inc(norm_step, 1)
                        pool.wait_ge(norm_step, n * NORM_STEPS + 2)
                        pool.tensor_tensor(norm[:, 2, :], norm[:, 1, :], moments[:, :, 1], ALU.mult) \
                            .then_inc(norm_step, 1)
                        pool.wait_ge(norm_step, n * NORM_STEPS + 3)
                        alone(pool)
                        pool.tensor_scalar(norm[:, 3, :], norm[:, 2, :], float(C), 1e-24, ALU.mult, ALU.max) \
                            .then_inc(norm_step, 1)
                        pool.wait_ge(norm_step, n * NORM_STEPS + 4)
                        pool.tensor_tensor(norm[:, 4, :], norm[:, 3, :], power[:, :], ALU.pow) \
                            .then_inc(norm_step, 1)
                    elif stage == "skip":
                        pool.wait_ge(xn_ready, n + 1)
                        for t in range(CT):
                            ins = pool.tensor_tensor(skip[:, t, :], xn[:, t, :], b_proj[:, :], ALU.add)
                        ins.then_inc(skip_ready, 1)
                    elif stage == "qk":
                        t = arg
                        q4 = qk[:, t, :].rearrange("p (h s e) -> p h s e", s=2, e=D // 2)
                        s4 = swapped[:, :].rearrange("p (h s e) -> p h s e", s=2, e=D // 2)

                        def table(k, halves):
                            return rotary[:, c * CT + t, k, :].rearrange("p (h s e) -> p h s e", h=1, s=1) \
                                .to_broadcast((P, 2 * H, halves, D // 2))
                        pool.wait_ge(bank_drained[i], use + 2)
                        wait(pool, rot_ready, n * CT + t)
                        pool.tensor_tensor(s4[:, :, 0:1, :], q4[:, :, 1:2, :], table(2, 1), ALU.mult)
                        pool.tensor_tensor(s4[:, :, 1:2, :], q4[:, :, 0:1, :], table(1, 1), ALU.mult) \
                            .then_inc(rope_step, 1)
                        pool.wait_ge(rope_step, n * (2 * CT) + (2 * t + 1))
                        pool.tensor_tensor(q4, q4, table(0, 2), ALU.mult).then_inc(rope_step, 1)
                        pool.wait_ge(rope_step, n * (2 * CT) + (2 * t + 2))
                        wait(pool, hi_ready, n * CT + (t + 1 - CT))
                        def by_head(tile):
                            return tile.rearrange("p (g h d) -> p g h d", h=GH, d=D)
                        pool.tensor_tensor(rot[:, t, :].rearrange("p (g d h) -> p g h d", h=GH, d=D),
                                           by_head(qk[:, t, :]), by_head(swapped[:, :]), ALU.add) \
                            .then_inc(rot_ready, 1)
                    elif stage == "mask_turn":
                        wait(pool, rest_out, n * 16)
                        for t in range(CT):
                            ins = pool.tensor_tensor(rest[:, t, :], x[:, c % 2, t, :], b_rest[:, :], ALU.add)
                        ins.then_inc(rest_ready, 1)
                    elif stage == "middle":
                        t = arg
                        pool.wait_ge(mid_ready, n * CT + (t + 1))
                        wait(pool, parts_out[2], n * 16)
                        pool.tensor_tensor(parts[2][:, :, t * P:(t + 1) * P], left[:, :, :],
                                           parts[1][:, :, t * P:(t + 1) * P], ALU.subtract).then_inc(lo_ready, 1)
                    elif stage == "widen":
                        pool.wait_ge(v_in_done, gi * 16 + 16)
                        wait(pool, probs_used, (gi - 1) * NS + PROBS)
                        alone(pool)
                        pool.tensor_copy(v_aug[ag % 2][:, :, :, 0:D],
                                         v_in[:, :, :].rearrange("p t (h d) -> p t h d", d=D)) \
                            .then_inc(v_aug_ready, 1)
                    elif stage == "y2_stats":
                        wait(pool, rstd2_ready, n - 1)
                        pool.wait_ge(moments2_ready, n)
                        alone(pool)
                        pool.tensor_scalar(norm[:, 5, :], moments2[:, :, 1], 1e-5, None, ALU.add) \
                            .then_inc(norm2_step, 1)
                        pool.wait_ge(norm2_step, n)
                        pool.tensor_tensor(rstd2[:, :], norm[:, 5, :], power[:, :], ALU.pow) \
                            .then_inc(rstd2_ready, 1)

            run(pool, body)

        @block.scalar
        def _(act):
            act.sem_inc(bank_drained[0], 1)
            act.sem_inc(bank_drained[1], 1)
            act.sem_inc(ring_drained, RING)
            act.sem_inc(o_out, 1)
            act.wait_ge(weights_in, LOADS * 16)
            act.activation(ident_b[:, :], ident[:, :], ACT.Copy).then_inc(cast, 1)
            act.activation(pick[:, :], act_t[0:E, 1:5, :].rearrange("p m n -> p (m n)"), ACT.Copy) \
                .then_inc(cast, 1)
            for r in range(2):
                act.wait_ge(bank_filled[r], 1)
                act.activation(rot[0:H, r, :], bank_pair[r][0:H, :], ACT.Copy).then_inc(offsets_made, 1)
                act.wait_ge(offsets_made, r + 1)
                act.sem_inc(bank_drained[r], 1)
            act.wait_ge(bank_filled[0], 2)
            act.activation(w_qkv[:, :, 3 * C:QKV], bank_pair[0][:, 0:KC * E].rearrange("p (k e) -> p k e", e=E),
                           ACT.Copy).then_inc(cast, 1)
            act.wait_ge(cast, 3)
            act.sem_inc(bank_drained[0], 1)
            act.sem_inc(bank_drained[1], 1)
            act.wait_ge(offsets_out, 16)

            def body(stages, b, bank_n, ring_n):
                for stage, g, arg, banks, rings, needs in stages:
                    fb, c, n = chunk_of(b, g)
                    i, use = bank_use(bank_n, banks)
                    bank = bank_pair[i]
                    tile_n = ring_n[0] + rings
                    scores = ring[(rings + ring_n[1]) % RING]
                    ab, ag, gi = next_group(b, g)
                    if stage == "score":
                        s, h = arg
                        if s in BIASED:
                            act.wait_ge(ring_biased, b * (NG * GH * len(BIASED))
                                        + (g * GH * len(BIASED) + BIASED.index(s) * GH + h + 1))
                        else:
                            act.wait_ge(ring_filled, tile_n + 1)
                        if h == 0:
                            act.wait_ge(probs_used, b * (NG * NS) + (g * NS + s + 1))
                        width = STEPS[s][2]
                        act.activation(probs[:, (g * NS + s) % PROBS, h, 0:width],
                                       scores[:, 0:width], ACT.Exp,
                                       scale=float(D) ** -0.5).then_inc(ring_drained, 1)
                    elif stage == "o_out":
                        k = b * (2 * NG) + (2 * g + arg)
                        act.wait_ge(probs_used, b * (NG * NS) + (g * NS + LAST_STEP[arg] + 1 + PROBS))
                        act.wait_ge(inv_ready, k + 1)
                        act.activation(o_sb[:, :], o_bank[:, :], ACT.Copy).then_inc(o_out, 1)
                    elif stage == "x_turn":
                        act.wait_ge(bank_filled[i], use + 1)
                        for t in range(CT):
                            ins = act.activation(xn_t[:, :, t * P:(t + 1) * P],
                                                 bank[:, t * C:(t + 1) * C].rearrange("p (k n) -> p k n", n=P),
                                                 ACT.Copy)
                        ins.then_inc(bank_drained[i], 1)
                    elif stage == "hidden":
                        act.wait_ge(ring_filled, tile_n + 1)
                        act.activation(hid_t[:, :], scores[:, 0:CH], ACT.Gelu,
                                       bias=b_hid[:, 0:1]).then_inc(ring_drained, 1)
                    elif stage == "gate":
                        act.wait_ge(bank_drained[i], use + 2)
                        act.activation(gate_th[:, :, :], gate_in[:, :, :], ACT.Tanh, scale=0.5) \
                            .then_inc(tanh_ready, 1)
                    elif stage == "choice":
                        act.wait_ge(chosen, n * CHOSEN_STEPS + 4)
                        act.activation(shares[:, :, :], below[:, :, :], ACT.Exp).then_inc(share_ready, 1)
                    elif stage == "qk_turn":
                        t = arg
                        act.wait_ge(bank_filled[i], use + 1)
                        wait(act, parts_out[0], n * 16)
                        act.activation(parts[0][:, :, t * P:(t + 1) * P],
                                       bank[:, :].rearrange("p (q n) -> p q n", n=P), ACT.Copy) \
                            .then_inc(hi_ready, 1)
                    elif stage == "middle":
                        t = arg
                        j, turned = bank_use(bank_n, needs)
                        act.wait_ge(bank_drained[j], turned + 2)
                        wait(act, parts_out[1], n * 16)
                        act.activation(parts[1][:, :, t * P:(t + 1) * P], left[:, :, :], ACT.Copy) \
                            .then_inc(mid_ready, 1)
                    elif stage == "mask_turn":
                        act.wait_ge(bank_filled[i], use + 1)
                        act.activation(others_t[:, :], bank[0:E, 0:CH], ACT.Copy).then_inc(bank_drained[i], 1)
                    elif stage == "shift_turn":
                        act.wait_ge(bank_filled[i], use + 1)
                        wait(act, shift_in, gi * 16)
                        act.activation(shift_t[:, :], bank[:, :].bitcast(BF16)[0:3 * GH * NT, 0:P], ACT.Copy) \
                            .then_inc(bank_drained[i], 1)
                    elif stage == "neurons" and arg[1] == N_PIECES - 1:
                        if g == -LEAD and arg[0] == 0:
                            act.wait_ge(columns_in, LATE_LOADS * 16)
                        act.wait_ge(ring_filled, tile_n + 1)
                        for m in range(N_PIECES):
                            mm = arg[0] * N_PIECES + m
                            ins = act.activation(act_t[:, mm, :], scores[:, m * CH:(m + 1) * CH],
                                                 ACT.Gelu, bias=b_cols[:, mm:mm + 1])
                        ins.then_inc(ring_drained, 1)
                    elif stage == "y_turn":
                        act.wait_ge(bank_filled[i], use + 1)
                        for t in range(CT):
                            ins = act.activation(y_t[:, :, t * P:(t + 1) * P],
                                                 bank[:, t * C:(t + 1) * C].rearrange("p (k n) -> p k n", n=P),
                                                 ACT.Copy)
                        ins.then_inc(bank_drained[i], 1)

            run(act, body)

        @block.tensor
        def _(pe):
            pe.wait_ge(weights_in, LOADS * 16)
            pe.wait_ge(filled, FILLS)
            for r in range(2):
                pe.wait_ge(bank_drained[r], 1)
                pe.matmul(bank_pair[r][0:H, :], y2[0:BUCKETS + 1, 0, 0:H], qk[0:BUCKETS + 1, r, :],
                          start=True, stop=True).then_inc(bank_filled[r], 1)
            pe.wait_ge(bank_drained[0], 2)
            pe.wait_ge(embedded, 4)
            for k in range(KC):
                ins = pe.transpose(bank_pair[0][:, k * E:(k + 1) * E], y2n[0:E, 1, k * P:(k + 1) * P],
                                   ident[0:E, 0:E])
            ins.then_inc(bank_filled[0], 1)
            pe.wait_ge(cast, 3)
            pe.nop().then_inc(bank_filled[1], 1)
            pe.sem_inc(probs_used, PROBS)

            def body(stages, b, bank_n, ring_n):
                for stage, g, arg, banks, rings, needs in stages:
                    fb, c, n = chunk_of(b, g)
                    i, use = bank_use(bank_n, banks)
                    bank = bank_pair[i]
                    tile_n = ring_n[0] + rings
                    scores = ring[(rings + ring_n[1]) % RING]
                    ab, ag, gi = next_group(b, g)
                    G = b * NG + g
                    if stage in BANKED | {"qk_begun", "project_begun"} and not (stage == "columns" and arg > 0):
                        pe.wait_ge(bank_drained[i], use + 1)
                    if NEEDS.get(stage) and stage not in ("y2_stats", "choose") and not (stage == "neurons" and arg[1] > 0):
                        j, needed = bank_use(bank_n, needs)
                        pe.wait_ge(bank_drained[j], needed + 2)
                    if stage == "score":
                        s, h = arg
                        pe.wait_ge(ring_drained, tile_n + 1)
                        if s == 0 and h == 0:
                            pe.wait_ge(shift_in, G * 16 + 16)
                        half, blocks, _ = STEPS[s]
                        for kb, q0, c0 in blocks:
                            w = (half + 1) * HALF - q0
                            ins = pe.matmul(scores[:, c0:c0 + w],
                                            stack_k[g % 2][:, h, kb * P:(kb + 1) * P],
                                            stack_q[g % 2][:, h, q0:q0 + w], start=True, stop=True)
                        ins.then_inc(ring_filled, 1)
                    elif stage == "pv":
                        s = arg
                        half, blocks, _ = STEPS[s]
                        if s == 0:
                            pe.wait_ge(v_aug_ready, G + 1)
                        if s in (0, LAST_STEP[0] + 1):
                            pe.wait_ge(o_out, b * (2 * NG) + (2 * g + half + 1))
                        pe.wait_ge(ring_drained, ring_n[0] + (needs + (1 + RING))) 
                        for kb, q0, c0 in blocks:
                            w = (half + 1) * HALF - q0
                            for h in range(GH):
                                ins = pe.matmul(o_bank[32 * h:32 * h + 32, HALF - w:HALF],
                                                v_aug[g % 2][:, kb, h, :], probs[:, (g * NS + s) % PROBS, h, c0:c0 + w],
                                                start=(kb == 0), stop=(kb == 4 * half + 3))
                        ins.then_inc(probs_used, 1)
                    elif stage == "row":
                        h, k = arg
                        qb, part = ROWS[k]
                        i = gi * (GH * len(ROWS)) + (h * len(ROWS) + k)
                        if h == 0 and k == 0:
                            pe.wait_ge(stack_in[ag % 2], (ab * (NG // 2) + (ag // 2 + 1)) * (2 * len(RUNS) * 16))
                        pe.wait_ge(rows_drained, i + 1)
                        tile = row_ring[(h * len(ROWS) + k) % 2]
                        q = stack_q[ag % 2][0:STACK, h, qb * P:(qb + 1) * P]
                        keys = stack_k[ag % 2][0:STACK, h, :]
                        far = max(qb - 1, 0) * P
                        if part == 0:
                            ins = pe.matmul(tile[:, 0:(qb + 1) * P - far], q, keys[:, far:(qb + 1) * P],
                                            start=True, stop=True)
                            if far:
                                w = min(far, 2 * P)
                                ins = pe.matmul(tile[:, 2 * P:2 * P + w], q, keys[:, 0:w], start=True, stop=True)
                        else:
                            ins = pe.matmul(tile[:, 0:far - 2 * P], q, keys[:, 2 * P:far], start=True, stop=True)
                        ins.then_inc(rows_filled, 1)
                    elif stage == "x_turn":
                        pe.wait_ge(xn_ready, n + 1)
                        for t in range(CT):
                            for k in range(KC):
                                ins = pe.transpose(bank[:, (t * KC + k) * P:(t * KC + k + 1) * P],
                                                   xn[:, t, k * P:(k + 1) * P], ident[:, :])
                        ins.then_inc(bank_filled[i], 1)
                    elif stage in ("qk_begun", "qk", "v"):
                        cols = slice(2 * C, QKV) if stage == "v" else slice(0, 2 * C)
                        for k in {"qk_begun": (0,), "qk": (1,), "v": (0, 1)}[stage]:
                            ins = pe.matmul(bank[:, 0:cols.stop - cols.start],
                                            xn_t[:, k, arg * P:(arg + 1) * P], w_qkv[:, k, cols],
                                            start=(k == 0), stop=(k == KC - 1))
                        if stage != "qk_begun":
                            ins.then_inc(bank_filled[i], 1)
                    elif stage == "hidden":
                        pe.wait_ge(ring_drained, tile_n + 1)
                        for k in range(KC):
                            ins = pe.matmul(scores[:, 0:CH], w_hid[:, k, :], xn_t[:, k, :],
                                            start=(k == 0), stop=(k == KC - 1))
                        ins.then_inc(ring_filled, 1)
                    elif stage == "gate":
                        pe.wait_ge(ring_drained, ring_n[0] + (needs + (1 + RING)))
                        for t in range(CT):
                            ins = pe.matmul(bank[:, t * E:(t + 1) * E], hid_t[:, t * P:(t + 1) * P],
                                            w_gate[:, :], start=True, stop=True)
                        ins.then_inc(bank_filled[i], 1)
                    elif stage == "qk_turn":
                        pe.wait_ge(rot_ready, n * CT + (arg + 1))
                        for q in range(2 * KC):
                            ins = pe.transpose(bank[:, q * P:(q + 1) * P], rot[:, arg, q * P:(q + 1) * P],
                                               ident[:, :])
                        ins.then_inc(bank_filled[i], 1)
                    elif stage == "mask_turn":
                        pe.wait_ge(chosen, n * CHOSEN_STEPS + 7)
                        for t in range(CT):
                            ins = pe.transpose(bank[0:E, t * P:(t + 1) * P], others[:, t, :], ident[:, :])
                        ins.then_inc(bank_filled[i], 1)
                    elif stage == "shift_turn":
                        pe.wait_ge(shift_step, gi * 6 + 6)
                        pe.transpose(bank[:, :].bitcast(BF16)[0:3 * GH * NT, 0:P],
                                     shift_p[:, :, :].rearrange("p r j -> p (r j)"), ident_b[:, :]) \
                            .then_inc(bank_filled[i], 1)
                    elif stage == "neurons":
                        part, m = arg
                        if g == -LEAD and arg == (0, 0):
                            pe.wait_ge(columns_in, LATE_LOADS * 16)
                        if m == 0:
                            pe.wait_ge(ring_drained, tile_n + 1)
                        mm = part * N_PIECES + m
                        dst = scores[:, m * CH:(m + 1) * CH]
                        for k in range(KC):
                            pe.matmul(dst, w_cols[:, k, mm * P:(mm + 1) * P], xn_t[:, k, :],
                                      start=(k == 0), stop=False)
                        ins = pe.matmul(dst, pick[:, mm * P:(mm + 1) * P], others_t[:, :],
                                        start=False, stop=True)
                        if m == N_PIECES - 1:
                            ins.then_inc(ring_filled, 1)
                    elif stage == "columns":
                        if arg == 0:
                            pe.wait_ge(ring_drained, tile_n + RING)
                        t, part = divmod(arg, C_PIECES // CT)
                        for m in range(part * M_PIECE, (part + 1) * M_PIECE):
                            ins = pe.matmul(bank[:, t * C:(t + 1) * C], act_t[:, m, t * P:(t + 1) * P],
                                            w_proj[:, m, :], start=(m == 0), stop=(m == EM - 1))
                        if arg == C_PIECES - 1:
                            ins.then_inc(bank_filled[i], 1)
                    elif stage == "o_turn":
                        pe.wait_ge(o_out, b * (2 * NG) + (2 * g + arg + 2))
                        for q in range(4):
                            ins = pe.transpose(bank[:, q * P:(q + 1) * P], o_sb[:, q * P:(q + 1) * P], ident[:, :])
                        ins.then_inc(bank_filled[i], 1)
                    elif stage == "y_turn":
                        for t in range(CT):
                            for k in range(KC):
                                ins = pe.transpose(bank[:, (t * KC + k) * P:(t * KC + k + 1) * P],
                                                   y[:, arg * CT + t, k * P:(k + 1) * P], ident[:, :])
                        ins.then_inc(bank_filled[i], 1)
                    elif stage in ("project_begun", "project"):
                        for t in ((0,) if stage == "project_begun" else (1,)):
                            for k in range(KC):
                                ins = pe.matmul(bank[:, t * C:(t + 1) * C], y_t[:, k, t * P:(t + 1) * P],
                                                w_out[:, k, :], start=(k == 0), stop=(k == KC - 1))
                        if stage == "project":
                            ins.then_inc(bank_filled[i], 1)

            run(pe, body)

        @block.vector
        def _(dve):
            dve.sem_inc(rows_drained, 2)
            dve.sem_inc(inv_ready, 1)
            dve.wait_ge(weights_in, LOADS * 16)
            emb = act_t[0:E, 0, :]
            dve.tensor_tensor_reduce(y2n[0:E, 0, :], emb, emb, 1.0, 0.0, ALU.mult, ALU.add,
                                     norm[0:E, 0, 0:1]).then_inc(embedded, 1)
            dve.wait_ge(embedded, 3)
            dve.tensor_scalar(y2n[0:E, 1, :], emb, norm[0:E, 2, 0:1], None, ALU.mult).then_inc(embedded, 1)
            dve.wait_ge(filled, FILLS)
            dve.wait_ge(bank_filled[0], 2)
            dve.wait_ge(bank_filled[1], 1)

            def each(col):
                return col.rearrange("p (t o) -> p t o", o=1).to_broadcast((P, CT, E))

            def body(stages, b, bank_n, ring_n):
                for stage, g, arg, banks, rings, needs in stages:
                    fb, c, n = chunk_of(b, g)
                    i, use = bank_use(bank_n, banks)
                    bank = bank_pair[i]
                    tile_n = ring_n[0] + rings
                    scores = ring[(rings + ring_n[1]) % RING]
                    ab, ag, gi = next_group(b, g)
                    if stage == "score":
                        s, h = arg
                        if s not in BIASED:
                            continue
                        dve.wait_ge(ring_filled, tile_n + 1)
                        near = near_cols[:, g * GH + h, :]
                        tile = scores
                        ins = (dve.tensor_tensor(tile[:, 0:P], tile[:, 0:P], near[:, P:2 * P], ALU.add)
                               if s == 6 else
                               dve.tensor_tensor(tile[:, 0:2 * P], tile[:, 0:2 * P], near, ALU.add))
                        if s in LAST_STEP:
                            ins = dve.tensor_tensor(tile[:, 2 * P:3 * P], tile[:, 2 * P:3 * P], near[:, 0:P],
                                                    ALU.add)
                        ins.then_inc(ring_biased, 1)
                    elif stage == "row":
                        h, k = arg
                        qb, part = ROWS[k]
                        i = gi * (GH * len(ROWS)) + (h * len(ROWS) + k)
                        tile = row_ring[(h * len(ROWS) + k) % 2]
                        at = h * NT + qb
                        far = max(qb - 1, 0) * P
                        if g < 0 and h == 0 and k == 0:
                            dve.wait_ge(near_in, 32)
                        if h == 0 and k == 0:
                            wait(dve, shift_step, gi * 6)
                            alone(dve)
                        dve.wait_ge(rows_filled, i + 1)
                        if part == 0:
                            if far:
                                w = min(far, 2 * P)
                                dve.tensor_reduce(maxima[:, 1, at:at + 1], tile[:, 2 * P:2 * P + w], AX.X, ALU.max)
                            w = (qb + 1) * P - far
                            if not far:
                                alone(dve)
                            dve.tensor_tensor_reduce(tile[:, 0:w], tile[:, 0:w],
                                                     near_rows[:, ag * GH + h, 2 * P - w:2 * P], 1.0, LOWEST,
                                                     ALU.add, ALU.max, maxima[:, 0, at:at + 1]) \
                                .then_inc(rows_drained, 1)
                        else:
                            dve.tensor_reduce(maxima[:, 2, at:at + 1], tile[:, 0:far - 2 * P], AX.X, ALU.max) \
                                .then_inc(rows_drained, 1)
                    elif stage == "shift":
                        step = lambda k: dve.wait_ge(shift_step, gi * 6 + k)
                        dve.wait_ge(rows_drained, gi * (GH * len(ROWS)) + (GH * len(ROWS) + 2))
                        dve.tensor_reduce(shift[:, :], maxima[:, :, :].rearrange("p k j -> p j k"), AX.X, ALU.max,
                                          negate=True).then_inc(shift_step, 1)
                        step(1)
                        dve.tensor_copy(shift_p[:, 0, :], shift[:, :]).then_inc(shift_step, 1)
                        step(2)
                        dve.tensor_tensor(shift_l[:, 0, :], shift[:, :], shift_p[:, 0, :], ALU.subtract) \
                            .then_inc(shift_step, 1)
                        step(3)
                        dve.tensor_copy(shift_p[:, 1, :], shift_l[:, 0, :]).then_inc(shift_step, 1)
                        step(4)
                        dve.tensor_tensor(shift_l[:, 1, :], shift_l[:, 0, :], shift_p[:, 1, :], ALU.subtract) \
                            .then_inc(shift_step, 1)
                        step(5)
                        dve.tensor_copy(shift_p[:, 2, :], shift_l[:, 1, :]).then_inc(shift_step, 1)
                    elif stage == "o_turn":
                        k = b * (2 * NG) + (2 * g + arg)
                        o4 = bank[:, :].rearrange("p (i h e) -> p i h e", h=GH, e=32)
                        dve.wait_ge(bank_filled[i], use + 1)
                        dve.reciprocal(inv[:, :, :], o4[:, :, :, D]).then_inc(inv_ready, 1)
                        dve.wait_ge(inv_ready, k + 2)
                        dst = y[:, arg * 4:(arg + 1) * 4, g * GH * D:(g + 1) * GH * D]
                        dve.tensor_tensor(dst.rearrange("p i (h d) -> p i h d", d=D), o4[:, :, :, 0:D],
                                          inv[:, :, :].rearrange("p i (h o) -> p i h o", o=1)
                                          .to_broadcast((P, 4, GH, D)), ALU.mult).then_inc(bank_drained[i], 1)
                    elif stage == "stats":
                        dve.wait_ge(x_in[c % 2], (fb * (NC // 2) + (c // 2 + 1)) * 16)
                        for t in range(CT):
                            ins = dve.bn_stats(stats[:, t, :], x[:, c % 2, t, :])
                        ins.then_inc(stats_done, 1)
                        dve.wait_ge(stats_done, n + 1)
                        alone(dve)
                        for t in range(CT):
                            ins = dve.bn_aggr(moments[:, t, :], stats[:, t, :])
                        ins.then_inc(moments_ready, 1)
                    elif stage == "center":
                        dve.wait_ge(rstd_ready, n + 1)
                        wait(dve, skip_ready, n)
                        for t in range(CT):
                            ins = dve.tensor_scalar(xn[:, t, :], x[:, c % 2, t, :], moments[:, t, 0:1],
                                                    rstd[:, t:t + 1], ALU.subtract, ALU.mult)
                        ins.then_inc(xn_ready, 1)
                    elif stage == "qk":
                        dve.wait_ge(bank_filled[i], use + 1)
                        wait(dve, rot_ready, n * CT + (arg + 1 - CT))
                        dve.tensor_tensor(qk[:, arg, :], bank[:, :], b_qkv[:, 0:2 * C], ALU.add) \
                            .then_inc(bank_drained[i], 1)
                    elif stage == "v":
                        dve.wait_ge(bank_filled[i], use + 1)
                        wait(dve, v_out, n * 16)
                        dve.tensor_tensor(v[:, arg, :], bank[:, 0:C], b_qkv[:, 2 * C:3 * C], ALU.add) \
                            .then_inc(v_ready, 1)
                        dve.wait_ge(norm_step, n * NORM_STEPS + 5)
                        dve.tensor_scalar(like[:, arg, :], bank[:, C:C + E], norm[:, 4, arg:arg + 1], 0.5,
                                          ALU.mult, ALU.add).then_inc(bank_drained[i], 1)
                    elif stage == "gate":
                        dve.wait_ge(bank_filled[i], use + 1)
                        dve.tensor_tensor(gate_in[:, :, :], bank[:, 0:CT * E].rearrange("p (t e) -> p t e", e=E),
                                          b_gate[:, :].rearrange("p (o e) -> p o e", o=1)
                                          .to_broadcast((P, CT, E)), ALU.add).then_inc(bank_drained[i], 1)
                    elif stage == "choose":
                        step = lambda k: dve.wait_ge(chosen, n * CHOSEN_STEPS + k)
                        dve.wait_ge(tanh_ready, n + 1)
                        j, liked = bank_use(bank_n, needs)
                        dve.wait_ge(bank_drained[j], liked + 2)
                        dve.scalar_tensor_tensor(out=logits[:, :, :], in0=gate_th[:, :, :], scalar=0.5,
                                                 in1=like[:, :, :], op0=ALU.mult, op1=ALU.add).then_inc(chosen, 1)
                        step(1)
                        dve.tensor_reduce(top[:, :], logits[:, :, :], AX.X, ALU.max).then_inc(chosen, 1)
                    elif stage == "tie":
                        step = lambda k: dve.wait_ge(chosen, n * CHOSEN_STEPS + k)
                        step(2)
                        dve.tensor_tensor(tied[:, :, :], logits[:, :, :], each(top[:, :]), ALU.is_equal) \
                            .then_inc(chosen, 1)
                        dve.tensor_tensor(below[:, :, :], logits[:, :, :], each(top[:, :]), ALU.subtract) \
                            .then_inc(chosen, 1)
                        step(3)
                        dve.tensor_tensor(ranked[:, :, :], tied[:, :, :],
                                          rank[:, :].rearrange("p (o e) -> p o e", o=1).to_broadcast((P, CT, E)),
                                          ALU.mult).then_inc(chosen, 1)
                    elif stage == "choice":
                        step = lambda k: dve.wait_ge(chosen, n * CHOSEN_STEPS + k)
                        step(5)
                        dve.tensor_reduce(first[:, :], ranked[:, :, :], AX.X, ALU.max).then_inc(chosen, 1)
                        step(6)
                        dve.tensor_tensor(others[:, :, :], ranked[:, :, :], each(first[:, :]), ALU.not_equal) \
                            .then_inc(chosen, 1)
                    elif stage == "mask_turn":
                        dve.wait_ge(share_ready, n + 1)
                        dve.tensor_reduce(total[:, :], shares[:, :, :], AX.X, ALU.add).then_inc(chosen, 1)
                        dve.wait_ge(chosen, n * CHOSEN_STEPS + 8)
                        dve.reciprocal(weight[:, :], total[:, :]).then_inc(weight_ready, 1)
                    elif stage == "left":
                        i, use = bank_use(bank_n, needs)
                        bank = bank_pair[i]
                        dve.wait_ge(hi_ready, n * CT + (arg + 1))
                        wait(dve, lo_ready, n * CT + arg)
                        dve.tensor_tensor(left[:, :, :], bank[:, :].rearrange("p (q n) -> p q n", n=P),
                                          parts[0][:, :, arg * P:(arg + 1) * P], ALU.subtract) \
                            .then_inc(bank_drained[i], 1)
                    elif stage == "columns" and arg == C_PIECES - 1:
                        dve.wait_ge(bank_filled[i], use + 1)
                        dve.wait_ge(weight_ready, n)
                        dve.wait_ge(skip_ready, n)
                        for t in range(CT):
                            ins = dve.scalar_tensor_tensor(out=y2[:, t, :], in0=bank[:, t * C:(t + 1) * C],
                                                           scalar=weight[:, t:t + 1], in1=skip[:, t, :],
                                                           op0=ALU.mult, op1=ALU.add)
                        ins.then_inc(bank_drained[i], 1)
                    elif stage == "y2_stats":
                        i, use = bank_use(bank_n, needs)
                        dve.wait_ge(bank_drained[i], use + 2)
                        for t in range(CT):
                            ins = dve.bn_stats(stats2[:, t, :], y2[:, t, :])
                        ins.then_inc(stats2_done, 1)
                        dve.wait_ge(stats2_done, n)
                        alone(dve)
                        for t in range(CT):
                            ins = dve.bn_aggr(moments2[:, t, :], stats2[:, t, :])
                        ins.then_inc(moments2_ready, 1)
                    elif stage == "finish":
                        dve.wait_ge(rstd2_ready, n)
                        wait(dve, rest_all, n - 1)
                        for t in range(CT):
                            ins = dve.tensor_scalar(y2n[:, t, :], y2[:, t, :], moments2[:, t, 0:1],
                                                    rstd2[:, t:t + 1], ALU.subtract, ALU.mult)
                        ins.then_inc(y2n_ready, 1)
                    elif stage == "project":
                        dve.wait_ge(bank_filled[i], use + 1)
                        dve.wait_ge(rest_in_done[arg % 2], projected(b, g) * (NC // 2 * 16) + (arg // 2 + 1) * 16)
                        sum_ = result[:, arg % 2].rearrange("p t n -> p (t n)")
                        dve.tensor_tensor(sum_, bank[:, :], sum_, ALU.add) \
                            .then_inc(bank_drained[i], 1)

            run(dve, body)


LOADS = 21
LATE_LOADS = KC + 3
FILLS = 9


_INS = {
    "x": "L0_attn_x", "Wq": "L0_attn_Wq", "bq": "L0_attn_bq", "Wk": "L0_attn_Wk", "bk": "L0_attn_bk",
    "Wv": "L0_attn_Wv", "bv": "L0_attn_bv", "Wp": "L0_attn_Wp", "bp": "L0_attn_bp",
    "rel_bias_table": "L0_attn_rel_bias_table", "col_emb": "L0_ffn_col_emb", "gate_w1": "L0_ffn_gate_w1",
    "gate_b1": "L0_ffn_gate_b1", "gate_w2": "L0_ffn_gate_w2", "gate_b2": "L0_ffn_gate_b2",
    "W_cols": "L0_ffn_W_cols", "b_cols": "L0_ffn_b_cols", "proj_w": "L0_ffn_proj_w",
    "proj_b": "L0_ffn_proj_b", "ln_g": "L0_ffn_ln_g", "ln_b": "L0_ffn_ln_b",
}


def shape_constants():
    f = np.float32
    freq = f(1.0) / f(10000.0) ** (np.arange(0, D, 2, dtype=f) / f(D))
    angle = np.arange(T, dtype=f)[:, None] * freq.astype(f)[None, :]
    cos, sin = np.cos(angle).astype(f), np.sin(angle).astype(f)
    rotary = np.stack([cos, sin, -sin], axis=1).reshape(NT, P, 3, D // 2).transpose(1, 0, 2, 3)
    n = np.arange(N_OFF) - P
    exact = BUCKETS // 2
    large = exact + (np.log(np.maximum(n, 1).astype(f) / f(exact)) / f(np.log(128 / exact)) * f(BUCKETS - exact)) \
        .astype(np.int32)
    bucket = np.where(n < exact, np.maximum(n, 0), np.minimum(large, BUCKETS - 1))
    picks = np.zeros((BUCKETS + 1, N_OFF), f)
    ok = n >= 0
    picks[bucket[ok], np.nonzero(ok)[0]] += 1
    picks[BUCKETS - 1, ok] -= 1
    picks[BUCKETS, ~ok] = 1
    assert not picks[:, n >= P + 1].any()
    neuron = np.arange(E * N) // N
    return {
        "ident": np.eye(P, dtype=f),
        "rank": (E - np.arange(E)).astype(f),
        "rotary": np.ascontiguousarray(rotary),
        "offset_picks": np.ascontiguousarray(np.stack([picks, picks[:, ::-1]], axis=1)),
        "pick": np.where(np.arange(E)[:, None] == neuron[None, :], f(OFF), f(0)).astype(f),
    }


def kernel(**inputs):
    import concourse.bacc as _bacc
    from concourse.bass_utils import run_bass_kernel_spmd as _run

    nc = _bacc.Bacc("TRN2", target_bir_lowering=False, num_devices=1)
    arrays, args = {}, {}
    given = {k: np.ascontiguousarray(inputs[name]) for k, name in _INS.items()}
    for name, arr in list(given.items()) + list(shape_constants().items()):
        arrays[f"in_{name}_dram"] = arr
        args[name] = nc.dram_tensor(f"in_{name}_dram", arr.shape, mybir.dt.from_np(arr.dtype),
                                    kind="ExternalInput").ap()
    out = nc.dram_tensor("out_0_dram", (B, T, C), F32, kind="ExternalOutput").ap()
    layer_kernel(nc, args, out)
    r = _run(nc, [arrays], core_ids=[0])
    return r.results[0]["out_0_dram"]
```
